# Optimizing a Trainium2 kernel written in Bass

```python
import numpy as np
import jax
import jax.numpy as jnp

def _softmax(x, axis=-1):
    return jax.nn.softmax(x, axis=axis)

def _gelu(x):
    return jax.nn.gelu(x, approximate=True)

def _silu(x):
    return jax.nn.silu(x)

def _sigmoid(x):
    return jax.nn.sigmoid(x)

def _layernorm(x, axis=-1, eps=1e-05):
    m = jnp.mean(x, axis=axis, keepdims=True)
    v = jnp.var(x, axis=axis, keepdims=True)
    return (x - m) / jnp.sqrt(v + eps)

def _scatter_add(tgt, idx, src, axis=0):
    return tgt.at[idx].add(src)

def _segment_sum(src, seg, n):
    return jax.ops.segment_sum(src, seg, n)
kernel_name = 'mk_macaron_d1_jaxref_r8_068b1b'

def setup_inputs(seed: int=0):
    np.random.seed(seed)
    _w = jnp.asarray

    def _L0_attn_setup():
        import jax, jax.numpy as jnp
        import numpy as np
        HEADS = 16
        PHI = (1.0 + np.sqrt(5.0)) / 2.0

        def phi_bias(L):
            pos = jnp.arange(L, dtype=jnp.float32) * PHI % 1.0
            dist = jnp.abs(pos[:, None] - pos[None, :])
            return jnp.log(jnp.exp(-dist) + 1e-08)
        key = jax.random.key(seed)
        k1, k2, k3, k4 = jax.random.split(key, 4)
        B, L, D = (2, 256, 128)
        x = jax.random.normal(k1, (B, L, D), dtype=jnp.float32)
        w_qkv = jax.random.normal(k2, (D, 3 * D), dtype=jnp.float32) * D ** (-0.5)
        w_proj = jax.random.normal(k3, (D, D), dtype=jnp.float32) * D ** (-0.5)
        b_proj = jax.random.normal(k4, (D,), dtype=jnp.float32) * 0.01
        return {'x': x, 'w_qkv': w_qkv, 'w_proj': w_proj, 'b_proj': b_proj}
    _L0_attn_in = _L0_attn_setup()

    def _L0_ffn_setup():
        import jax, jax.numpy as jnp
        import numpy as np
        DIM = 128
        HIDDEN = 512
        E = 8
        B, S = (2, 512)
        key = jax.random.key(seed)
        ks = jax.random.split(key, 8)
        sd = 1.0 / np.sqrt(DIM)
        sh = 1.0 / np.sqrt(HIDDEN)
        return {'x': jax.random.normal(ks[0], (B, S, DIM), dtype=jnp.float32), 'router_w': jax.random.uniform(ks[1], (DIM, E), jnp.float32, -sd, sd), 'router_b': jax.random.uniform(ks[2], (E,), jnp.float32, -sd, sd), 'w1': jax.random.uniform(ks[3], (E, DIM, 2 * HIDDEN), jnp.float32, -sd, sd), 'b1': jax.random.uniform(ks[4], (E, 2 * HIDDEN), jnp.float32, -sd, sd), 'w2': jax.random.uniform(ks[5], (E, HIDDEN, DIM), jnp.float32, -sh, sh), 'b2': jax.random.uniform(ks[6], (E, DIM), jnp.float32, -sh, sh)}
    _L0_ffn_in = _L0_ffn_setup()
    _d = {'L0_attn_x': _L0_attn_in['x'], 'L0_attn_w_qkv': _L0_attn_in['w_qkv'], 'L0_attn_w_proj': _L0_attn_in['w_proj'], 'L0_attn_b_proj': _L0_attn_in['b_proj'], 'L0_ffn_router_w': _L0_ffn_in['router_w'], 'L0_ffn_router_b': _L0_ffn_in['router_b'], 'L0_ffn_w1': _L0_ffn_in['w1'], 'L0_ffn_b1': _L0_ffn_in['b1'], 'L0_ffn_w2': _L0_ffn_in['w2'], 'L0_ffn_b2': _L0_ffn_in['b2']}
    _x0 = _d['L0_attn_x']
    _d['L0_attn_x'] = jax.random.normal(jax.random.fold_in(jax.random.key(seed), 1), (4, 1024, 128), dtype=_x0.dtype)
    del _x0
    return _d

def reference(L0_attn_x, L0_attn_w_qkv, L0_attn_w_proj, L0_attn_b_proj, L0_ffn_router_w, L0_ffn_router_b, L0_ffn_w1, L0_ffn_b1, L0_ffn_w2, L0_ffn_b2):

    def _L0_attn_ref(x, w_qkv, w_proj, b_proj):
        import jax, jax.numpy as jnp
        import numpy as np
        HEADS = 16
        PHI = (1.0 + np.sqrt(5.0)) / 2.0

        def phi_bias(L):
            pos = jnp.arange(L, dtype=jnp.float32) * PHI % 1.0
            dist = jnp.abs(pos[:, None] - pos[None, :])
            return jnp.log(jnp.exp(-dist) + 1e-08)
        B, L, D = x.shape
        H = HEADS
        Dh = D // H
        scale = Dh ** (-0.5)
        qkv = (x @ w_qkv).reshape(B, L, 3, H, Dh)
        q = jnp.transpose(qkv[:, :, 0], (0, 2, 1, 3))
        k = jnp.transpose(qkv[:, :, 1], (0, 2, 1, 3))
        v = jnp.transpose(qkv[:, :, 2], (0, 2, 1, 3))
        attn = jnp.einsum('bhid,bhjd->bhij', q, k) * scale
        attn = attn + phi_bias(L)[None, None]
        attn = jax.nn.softmax(attn, axis=-1)
        out = jnp.einsum('bhij,bhjd->bhid', attn, v)
        out = jnp.transpose(out, (0, 2, 1, 3)).reshape(B, L, D)
        return out @ w_proj + b_proj

    def _L0_ffn_ref(x, router_w, router_b, w1, b1, w2, b2):
        import jax, jax.numpy as jnp
        import numpy as np
        DIM = 128
        HIDDEN = 512
        E = 8
        B, S = (2, 512)
        logits = jnp.einsum('bsd,de->bse', x, router_w) + router_b
        probs = jax.nn.softmax(logits, axis=-1)
        top1 = jnp.argmax(probs, axis=-1)
        out = jnp.zeros_like(x)
        for i in range(E):
            h = jnp.einsum('bsd,df->bsf', x, w1[i]) + b1[i]
            a, g = jnp.split(h, 2, axis=-1)
            y = jnp.einsum('bsh,hd->bsd', a * jax.nn.sigmoid(g), w2[i]) + b2[i]
            out = out + jnp.where((top1 == i)[..., None], y, 0.0)
        return out
    x = L0_attn_x
    x = x + 0.5 * _L0_ffn_ref(_layernorm(x, axis=-1), L0_ffn_router_w, L0_ffn_router_b, L0_ffn_w1, L0_ffn_b1, L0_ffn_w2, L0_ffn_b2)
    x = x + _L0_attn_ref(_layernorm(x, axis=-1), L0_attn_w_qkv, L0_attn_w_proj, L0_attn_b_proj)
    x = x + 0.5 * _L0_ffn_ref(_layernorm(x, axis=-1), L0_ffn_router_w, L0_ffn_router_b, L0_ffn_w1, L0_ffn_b1, L0_ffn_w2, L0_ffn_b2)
    return x

_drawn_inputs = setup_inputs


def setup_inputs(seed=0):
    import zlib

    import numpy as np

    out = dict(_drawn_inputs(seed))
    spreads = {}
    factors = {'L0_attn_b_proj': 3.85, 'L0_ffn_b1': 3.219}
    for name, (base, spread) in spreads.items():
        noise = np.random.default_rng([zlib.crc32(name.encode()), seed]).standard_normal(out[name].shape)
        drawn = base * np.exp(spread * noise) if base else spread * noise
        out[name] = jnp.asarray(drawn.astype(out[name].dtype))
    for name, factor in factors.items():
        out[name] = (out[name] * factor).astype(out[name].dtype)
    return out
```

```python
from contextlib import ExitStack

import concourse.bass as bass
from concourse import mybir

P = 128
D = 128
B, L = 4, 1024
NTOK = B * L
NT = NTOK // P
HEADS, DH = 16, 8
NHEAD = B * HEADS
E, HID = 8, 512
ET = NT + E
KT = L // P
HALF = 512
VW = DH + 1
COMBO = 9 * DH
BIAS0, BIASN = COMBO, 6 * KT
MAX0 = BIAS0 + BIASN
SROWS = MAX0
TROWS = MAX0 + 3
PBLK = L + P
NBUF = 4
LN_EPS = 1e-5

ALU = mybir.AluOpType
ACT = mybir.ActivationFunctionType
AX = mybir.AxisListType
F32 = mybir.dt.float32
BF16 = mybir.dt.bfloat16
I32 = mybir.dt.int32

C_ID, C_TRI, C_ONE, C_SEL, C_DIAG, C_IOTA, C_TILE, C_END = 0, 128, 256, 384, 416, 1440, 1448, 1488


class Mem:

    def __init__(self, nc, ctx):
        self.nc, self.ctx = nc, ctx

    def sb(self, name, shape, dt=F32):
        return self.ctx.enter_context(self.nc.sbuf_tensor(name, shape, dt))

    def ps(self, name, shape, dt=F32):
        return self.ctx.enter_context(self.nc.psum_tensor(name, shape, dt))

    def sem(self, name):
        return self.ctx.enter_context(self.nc.semaphore(name))


def phase_load(nc, d, g):
    with ExitStack() as ctx:
        m = Mem(nc, ctx)
        zero = m.sb("zero", [P, D])
        s_loaded, s_zero, s_cleared = m.sem("s_loaded"), m.sem("s_zero"), m.sem("s_cleared")
        block = ctx.enter_context(nc.Block())

        @block.sync
        def _(sp):
            sp.dma_start(g.x[:], d.x).then_inc(s_loaded, 16)
            sp.dma_start(g.const[:], d.const).then_inc(s_loaded, 16)
            sp.dma_start(g.wr[:], d.router_w).then_inc(s_loaded, 16)
            sp.dma_start(g.br[:], d.router_b.partition_broadcast(P)).then_inc(s_loaded, 16)
            sp.dma_start(g.wqkv[:], d.w_qkv).then_inc(s_loaded, 16)
            sp.dma_start(g.wproj[:], d.w_proj).then_inc(s_loaded, 16)
            sp.dma_start(g.bproj[:], d.b_proj.partition_broadcast(P)).then_inc(s_loaded, 16)
            sp.wait_ge(s_zero, 1)
            sp.dma_start(d.sorted.rearrange("(t p) d -> p t d", p=P),
                         zero[:].unsqueeze(1).to_broadcast([P, ET, D])).then_inc(s_cleared, 16)
            sp.wait_ge(s_loaded, 7 * 16)
            sp.wait_ge(s_cleared, 16)

        @block.gpsimd
        def _(pool):
            nc.gpsimd.memset(zero[:], 0.0).then_inc(s_zero, 1)


def phase_norm_stats(nc, g, tag):
    with ExitStack() as ctx:
        m = Mem(nc, ctx)
        stats = m.sb(f"stats{tag}", [P, 4, 6])
        mv = m.sb(f"mv{tag}", [P, 4, 2])
        s_var, s_std = m.sem(f"s_var{tag}"), m.sem(f"s_std{tag}")
        block = ctx.enter_context(nc.Block())

        @block.vector
        def _(dve):
            with dve.Fori(0, NT // 4) as i:
                for j in range(4):
                    nc.vector.bn_stats(stats[:, j, :], g.x[:, bass.ds(i * 512 + j * D, D)])
                dve.drain()
                for j in range(4):
                    nc.vector.bn_aggr(mv[:, j, :], stats[:, j, :])
                dve.drain()
                nc.vector.tensor_copy(g.mean[:, bass.ds(i * 4, 4)], mv[:, :, 0])
                nc.vector.tensor_scalar(g.var[:, bass.ds(i * 4, 4)], mv[:, :, 1], LN_EPS, None, ALU.add)
                dve.drain()
            dve.drain().then_inc(s_var, 1)
            dve.wait_ge(s_std, 1)
            nc.vector.reciprocal(g.rstd[:], g.std[:])

        @block.scalar
        def _(act):
            act.wait_ge(s_var, 1)
            nc.scalar.activation(g.std[:], g.var[:], ACT.Sqrt).then_inc(s_std, 1)


def normalise_group(nc, g, out, i, s):
    for j in range(4):
        last = nc.vector.tensor_scalar(
            out[:, s, j, :], g.x[:, bass.ds(i * 1024 + s * 512 + j * D, D)],
            g.mean[:, bass.ds(i * 8 + s * 4 + j, 1)], g.rstd[:, bass.ds(i * 8 + s * 4 + j, 1)],
            ALU.subtract, ALU.mult)
    return last


def phase_router(nc, g, tag):
    with ExitStack() as ctx:
        m = Mem(nc, ctx)
        xnb = m.sb(f"xnb{tag}", [P, 2, 4, D])
        xT = m.sb(f"xT{tag}", [P, 2, 512])
        psT = [m.ps(f"psT{tag}{s}", [P, 512]) for s in range(2)]
        psL = [m.ps(f"psL{tag}{s}", [P, 512]) for s in range(2)]
        s_xn, s_tp, s_xT = m.sem(f"s_xn{tag}"), m.sem(f"s_tp{tag}"), m.sem(f"s_xT{tag}")
        s_kept, s_lp, s_lg = m.sem(f"s_kept{tag}"), m.sem(f"s_lp{tag}"), m.sem(f"s_lg{tag}")
        block = ctx.enter_context(nc.Block())

        @block.vector
        def _(dve):
            def norm(i, s, first):
                if not first:
                    dve.wait_ge(s_tp, 2 * i + s - 1)
                    dve.wait_ge(s_kept, 2 * i + s - 1)
                normalise_group(nc, g, xnb, i, s).then_inc(s_xn, 1)

            def logits(i, s):
                dve.wait_ge(s_lp, 2 * i + s + 1)
                nc.vector.tensor_tensor(
                    g.logit[:, bass.ds(i * 64 + s * 32, 32)].rearrange("p (j e) -> p j e", e=E),
                    psL[s][:, 0:32].rearrange("p (j e) -> p j e", e=E),
                    g.br[:].unsqueeze(1).to_broadcast([P, 4, E]), ALU.add).then_inc(s_lg, 1)

            norm(0, 0, True)
            norm(0, 1, True)
            with dve.Fori(0, B - 1) as i:
                for s in range(2):
                    norm(i + 1, s, False)
                    logits(i, s)
            for s in range(2):
                logits(B - 1, s)

        @block.tensor
        def _(pe):
            def group(i, s, first):
                pe.wait_ge(s_xn, 2 * i + s + 1)
                if not first:
                    pe.wait_ge(s_xT, 2 * i + s - 1)
                for j in range(4):
                    last = nc.tensor.transpose(psT[s][:, j * D:(j + 1) * D], xnb[:, s, j, :], g.ident)
                last.then_inc(s_tp, 1)
                pe.wait_ge(s_xT, 2 * i + s + 1)
                if not first:
                    pe.wait_ge(s_lg, 2 * i + s - 1)
                for j in range(4):
                    last = nc.tensor.matmul(psL[s][:, j * E:(j + 1) * E], xT[:, s, j * D:(j + 1) * D],
                                            g.wr[:], start=True, stop=True)
                last.then_inc(s_lp, 1)

            for s in range(2):
                group(0, s, True)
            with pe.Fori(1, B) as i:
                for s in range(2):
                    group(i, s, False)

        @block.scalar
        def _(act):
            def group(i, s, first):
                act.wait_ge(s_tp, 2 * i + s + 1)
                if not first:
                    act.wait_ge(s_lp, 2 * i + s - 1)
                nc.scalar.copy(xT[:, s, :], psT[s][:]).then_inc(s_xT, 1)
                nc.scalar.copy(g.xn[:, bass.ds(i * 1024 + s * 512, 512)],
                               xnb[:, s, :, :].rearrange("p j d -> p (j d)")).then_inc(s_kept, 1)

            for s in range(2):
                group(0, s, True)
            with act.Fori(1, B) as i:
                for s in range(2):
                    group(i, s, False)


def phase_route(nc, g, tag):
    with ExitStack() as ctx:
        m = Mem(nc, ctx)
        N = NT * E
        best = m.sb(f"best{tag}", [P, NT])
        eq = m.sb(f"eq{tag}", [P, NT, E])
        pick = m.sb(f"pick{tag}", [P, NT])
        hot = m.sb(f"hot{tag}", [P, E, NT])
        total = m.sb(f"total{tag}", [P, E, NT])
        incl = m.sb(f"incl{tag}", [P, E, NT])
        excl = m.sb(f"excl{tag}", [P, E, NT])
        ones = m.sb(f"ones{tag}", [P, N])
        row = m.sb(f"row{tag}", [P, E, NT])
        cnt = m.sb(f"cnt{tag}", [P, E])
        whole = m.sb(f"whole{tag}", [P, E], I32)
        pad = m.sb(f"pad{tag}", [P, E])
        end = m.sb(f"end{tag}", [P, E])
        off = m.sb(f"off{tag}", [P, E])
        posf = m.sb(f"posf{tag}", [P, NT])
        before = m.sb(f"before{tag}", [1, ET, E])
        eidf = m.sb(f"eidf{tag}", [1, ET])
        psR = m.ps(f"psR{tag}", [P, 512])
        psC = m.ps(f"psC{tag}", [P, 512])
        s_hot, s_rank = m.sem(f"s_hot{tag}"), m.sem(f"s_rank{tag}")
        block = ctx.enter_context(nc.Block())
        iota = g.const[:, C_IOTA:C_IOTA + E]
        lg = g.logit[:].rearrange("p (t e) -> p t e", e=E)

        @block.vector
        def _(dve):
            nc.vector.memset(ones[:], 1.0)
            nc.vector.tensor_reduce(best[:], lg, AX.X, ALU.max)
            dve.drain()
            nc.vector.tensor_tensor(eq[:], lg, best[:].unsqueeze(2).to_broadcast([P, NT, E]), ALU.is_equal)
            dve.drain()
            nc.vector.tensor_tensor(eq[:], eq[:], iota.unsqueeze(1).to_broadcast([P, NT, E]), ALU.mult)
            dve.drain()
            nc.vector.tensor_reduce(pick[:], eq[:], AX.X, ALU.min)
            dve.drain()
            nc.vector.tensor_tensor(hot[:].rearrange("p e t -> p t e"),
                                    iota.unsqueeze(1).to_broadcast([P, NT, E]),
                                    pick[:].unsqueeze(2).to_broadcast([P, NT, E]),
                                    ALU.is_equal).then_inc(s_hot, 1)
            dve.wait_ge(s_rank, 1)
            nc.vector.tensor_copy(total[:].rearrange("p e t -> p (e t)"), psC[:, 0:N])
            dve.drain()
            nc.vector.tensor_tensor_scan(incl[:].rearrange("p e t -> p (e t)"), ones[:],
                                         total[:].rearrange("p e t -> p (e t)"), 0.0, ALU.mult, ALU.add)
            dve.drain()
            nc.vector.tensor_tensor(excl[:], incl[:], total[:], ALU.subtract)
            dve.drain()
            nc.vector.tensor_tensor(cnt[:], incl[:, :, NT - 1], excl[:, :, 0], ALU.subtract)
            nc.vector.tensor_tensor(row[:].rearrange("p e t -> p (e t)"), psR[:, 0:N],
                                    excl[:].rearrange("p e t -> p (e t)"), ALU.add)
            dve.drain()
            nc.vector.tensor_scalar(pad[:], cnt[:], float(P - 1), None, ALU.add)
            dve.drain()
            nc.vector.tensor_copy(whole[:], pad[:])
            dve.drain()
            nc.vector.tensor_scalar(whole[:], whole[:], 7, 7, ALU.logical_shift_right,
                                    ALU.logical_shift_left)
            dve.drain()
            nc.vector.tensor_copy(pad[:], whole[:])
            dve.drain()
            nc.vector.tensor_tensor_scan(end[:], ones[:, 0:E], pad[:], 0.0, ALU.mult, ALU.add)
            dve.drain()
            nc.vector.tensor_tensor(off[:], end[:], pad[:], ALU.subtract)
            dve.drain()
            nc.vector.tensor_tensor(off[:], off[:], excl[:, :, 0], ALU.subtract)
            nc.vector.tensor_tensor(before[:], end[0:1, :].unsqueeze(1).to_broadcast([1, ET, E]),
                                    g.const[0:1, C_TILE:C_TILE + ET].unsqueeze(2).to_broadcast([1, ET, E]),
                                    ALU.is_le)
            dve.drain()
            nc.vector.tensor_tensor(row[:], row[:], off[:].unsqueeze(2).to_broadcast([P, E, NT]), ALU.add)
            nc.vector.tensor_reduce(eidf[:], before[:], AX.X, ALU.add)
            dve.drain()
            nc.vector.tensor_tensor(row[:], row[:], hot[:], ALU.mult)
            nc.vector.tensor_scalar(g.eid[:], eidf[:], float(E - 1), None, ALU.min)
            dve.drain()
            nc.vector.tensor_reduce(posf[:], row[:].rearrange("p e t -> p t e"), AX.X, ALU.add)
            dve.drain()
            nc.vector.tensor_copy(g.pos[:], posf[:])

        @block.tensor
        def _(pe):
            pe.wait_ge(s_hot, 1)
            flat = hot[:].rearrange("p e t -> p (e t)")
            nc.tensor.matmul(psR[:, 0:N], g.const[:, C_TRI:C_TRI + P], flat, start=True, stop=True)
            nc.tensor.matmul(psC[:, 0:N], g.const[:, C_ONE:C_ONE + P], flat, start=True,
                             stop=True).then_inc(s_rank, 1)


def phase_scatter(nc, d, g, tag):
    with ExitStack() as ctx:
        m = Mem(nc, ctx)
        s_put = m.sem(f"s_put{tag}")
        block = ctx.enter_context(nc.Block())

        @block.gpsimd
        def _(pool):
            for t in range(NT):
                pool.indirect_dma_start(
                    out=d.sorted, out_offset=bass.IndirectOffsetOnAxis(ap=g.pos[:, t:t + 1], axis=0),
                    in_=g.xn[:, t * D:(t + 1) * D], in_offset=None).then_inc(s_put, 16)
            pool.wait_ge(s_put, 16 * NT)


def phase_experts(nc, d, g, tag):
    with ExitStack() as ctx:
        m = Mem(nc, ctx)
        w1 = m.sb(f"w1{tag}", [P, E * 2 * HID])
        w2 = m.sb(f"w2{tag}", [P, E * HID])
        b1 = m.sb(f"b1{tag}", [P, E * 2 * HID])
        b2 = m.sb(f"b2{tag}", [P, E * D])
        xs = m.sb(f"xs{tag}", [P, 2, D])
        xsT = m.sb(f"xsT{tag}", [P, 2, P])
        gate = m.sb(f"gate{tag}", [P, 2, HID])
        sig = m.sb(f"sig{tag}", [P, 2, HID])
        up = m.sb(f"up{tag}", [P, 2, HID])
        hid = m.sb(f"hid{tag}", [P, 2, HID])
        hidT = m.sb(f"hidT{tag}", [P, 2, HID])
        y = m.sb(f"y{tag}", [P, 2, D])
        psA = [m.ps(f"psA{tag}{s}", [P, HID]) for s in range(2)]
        psG = [m.ps(f"psG{tag}{s}", [P, HID]) for s in range(2)]
        psX = m.ps(f"psX{tag}", [P, 512])
        psH = m.ps(f"psH{tag}", [P, 512])
        psY = m.ps(f"psY{tag}", [P, 512])
        S = {n: m.sem(f"s_{n}{tag}") for n in
             ("w", "xs", "xt", "xsT", "h", "gate", "sig", "up", "hid", "ht", "hidT", "yp", "y", "st")}
        s_xs = [m.sem(f"s_xs{tag}{s}") for s in range(2)]
        s_st = [m.sem(f"s_st{tag}{s}") for s in range(2)]
        block = ctx.enter_context(nc.Block())
        T = ET

        def steps(eng, step):
            for i in (-1, 0, 1):
                step(i, i % 2, i, i // 2)
            with eng.Fori(0, T // 2 - 2) as q:
                for s in range(2):
                    step(q * 2 + 2 + s, s, None, q + 1)
            for i in (T - 2, T - 1, T, T + 1):
                step(i, i % 2, i, i // 2)

        def live(at, lag):
            return at is None or 0 <= at - lag < T

        def later(at, lag, n):
            return at is None or at - lag >= n

        @block.sync
        def _(sp):
            sp.dma_start(w1[:], d.w1).then_inc(S["w"], 16)
            sp.dma_start(w2[:], d.w2).then_inc(S["w"], 16)
            sp.dma_start(b1[:], d.b1.partition_broadcast(P)).then_inc(S["w"], 16)
            sp.dma_start(b2[:], d.b2.partition_broadcast(P)).then_inc(S["w"], 16)

            def step(i, s, at, pair):
                if live(at, -1):
                    if later(at, -1, 2):
                        sp.wait_ge(S["xt"], i)
                    sp.dma_start(xs[:, 1 - s, :], d.sorted[bass.ds((i + 1) * P, P), :])\
                        .then_inc(s_xs[1 - s], 16)
                if live(at, 2):
                    sp.wait_ge(S["y"], i - 1)
                    sp.dma_start(d.ysorted[bass.ds((i - 2) * P, P), :], y[:, s, :]).then_inc(s_st[s], 16)
            steps(sp, step)
            for s in range(2):
                sp.wait_ge(s_st[s], 16 * (T // 2))

        @block.tensor
        def _(pe):
            pe.wait_ge(S["w"], 64)
            if True:
                def expert(i):
                    return pe.value_load(g.eid[0:1, bass.ds(i, 1)], min_val=0, max_val=E - 1)

                def step(i, s, at, pair):
                    if live(at, -1):
                        pe.wait_ge(s_xs[1 - s], (pair + 1 + s) * 16)
                        if later(at, -1, 1):
                            pe.wait_ge(S["xsT"], i + 1)
                        nc.tensor.transpose(psX[:, 0:P], xs[:, 1 - s, :], g.ident).then_inc(S["xt"], 1)
                    if live(at, 0):
                        e = expert(i)
                        pe.wait_ge(S["xsT"], i + 1)
                        if later(at, 0, 2):
                            pe.wait_ge(S["up"], i - 1)
                        nc.tensor.matmul(psG[s][:], xsT[:, s, :], w1[:, bass.ds(e * 2 * HID + HID, HID)],
                                         start=True, stop=True).then_inc(S["h"], 1)
                        nc.tensor.matmul(psA[s][:], xsT[:, s, :], w1[:, bass.ds(e * 2 * HID, HID)],
                                         start=True, stop=True).then_inc(S["h"], 1)
                    if live(at, 1):
                        pe.wait_ge(S["hid"], i)
                        if later(at, 1, 1):
                            pe.wait_ge(S["hidT"], i - 1)
                        for c in range(4):
                            last = nc.tensor.transpose(psH[:, c * P:(c + 1) * P],
                                                       hid[:, 1 - s, c * P:(c + 1) * P], g.ident)
                        last.then_inc(S["ht"], 1)
                    if live(at, 2):
                        e = expert(i - 2)
                        pe.wait_ge(S["hidT"], i - 1)
                        if later(at, 2, 1):
                            pe.wait_ge(S["y"], i - 2)
                        for c in range(4):
                            last = nc.tensor.matmul(psY[:, 0:D], hidT[:, s, c * P:(c + 1) * P],
                                                    w2[:, bass.ds(e * HID + c * P, P)],
                                                    start=(c == 0), stop=(c == 3))
                        last.then_inc(S["yp"], 1)
                steps(pe, step)

        @block.vector
        def _(dve):
            dve.wait_ge(S["w"], 64)

            def expert(i):
                return dve.value_load(g.eid[0:1, bass.ds(i, 1)], min_val=0, max_val=E - 1)

            def step(i, s, at, pair):
                if live(at, 0):
                    e = expert(i)
                    dve.wait_ge(S["h"], 2 * i + 1)
                    if later(at, 0, 2):
                        dve.wait_ge(S["sig"], i - 1)
                    nc.vector.tensor_tensor(gate[:, s, :], psG[s][:], b1[:, bass.ds(e * 2 * HID + HID, HID)],
                                            ALU.add).then_inc(S["gate"], 1)
                    dve.wait_ge(S["h"], 2 * i + 2)
                    nc.vector.tensor_tensor(up[:, s, :], psA[s][:], b1[:, bass.ds(e * 2 * HID, HID)],
                                            ALU.add).then_inc(S["up"], 1)
                if live(at, 2):
                    e = expert(i - 2)
                    dve.wait_ge(S["yp"], i - 1)
                    if later(at, 2, 2):
                        dve.wait_ge(s_st[s], (pair - 1) * 16)
                    nc.vector.tensor_tensor(y[:, s, :], psY[:, 0:D], b2[:, bass.ds(e * D, D)],
                                            ALU.add).then_inc(S["y"], 1)
                if live(at, 0):
                    dve.wait_ge(S["sig"], i + 1)
                    dve.wait_ge(S["up"], i + 1)
                    if later(at, 0, 2):
                        dve.wait_ge(S["ht"], i - 1)
                    nc.vector.tensor_tensor(hid[:, s, :], up[:, s, :], sig[:, s, :],
                                            ALU.mult).then_inc(S["hid"], 1)
            steps(dve, step)

        @block.scalar
        def _(act):
            def step(i, s, at, pair):
                if live(at, -1):
                    act.wait_ge(S["xt"], i + 2)
                    if later(at, -1, 2):
                        act.wait_ge(S["h"], 2 * i)
                    nc.scalar.copy(xsT[:, 1 - s, :], psX[:, 0:P]).then_inc(S["xsT"], 1)
                if live(at, 1):
                    act.wait_ge(S["ht"], i)
                    if later(at, 1, 2):
                        act.wait_ge(S["yp"], i - 2)
                    nc.scalar.copy(hidT[:, 1 - s, :], psH[:]).then_inc(S["hidT"], 1)
                if live(at, 0):
                    act.wait_ge(S["gate"], i + 1)
                    if later(at, 0, 2):
                        act.wait_ge(S["hid"], i - 1)
                    nc.scalar.activation(sig[:, s, :], gate[:, s, :], ACT.Sigmoid).then_inc(S["sig"], 1)
            steps(act, step)


def phase_gather(nc, d, g, tag, out):
    with ExitStack() as ctx:
        m = Mem(nc, ctx)
        s_got = [m.sem(f"s_got{tag}{n}") for n in range(NT // 4)]
        s_add, s_out = m.sem(f"s_add{tag}"), m.sem(f"s_out{tag}")
        block = ctx.enter_context(nc.Block())

        @block.gpsimd
        def _(pool):
            for t in range(NT):
                pool.indirect_dma_start(
                    out=g.xn[:, t * D:(t + 1) * D], out_offset=None, in_=d.ysorted,
                    in_offset=bass.IndirectOffsetOnAxis(ap=g.pos[:, t:t + 1], axis=0))\
                    .then_inc(s_got[t // 4], 16)

        @block.vector
        def _(dve):
            for n in range(NT // 4):
                dve.wait_ge(s_got[n], 64)
                at = slice(n * 512, (n + 1) * 512)
                nc.vector.scalar_tensor_tensor(out=g.x[:, at], in0=g.xn[:, at], scalar=0.5,
                                               in1=g.x[:, at], op0=ALU.mult, op1=ALU.add)\
                    .then_inc(s_add, 1)

        if out is not None:
            @block.sync
            def _(sp):
                with sp.Fori(0, NT // 4) as i:
                    sp.wait_ge(s_add, i + 1)
                    at = bass.ds(i * 512, 512)
                    sp.dma_start(out[:, at], g.x[:, at]).then_inc(s_out, 16)
                sp.wait_ge(s_out, 16 * (NT // 4))


def phase_qkv(nc, d, g):
    with ExitStack() as ctx:
        m = Mem(nc, ctx)
        xnb = m.sb("q_xnb", [P, 2, 4, D])
        xT = m.sb("q_xT", [P, 2, 512])
        f = m.sb("q_f", [P, 2, 2, 512])
        part = m.sb("q_part", [P, 2, 2, 3, 512], BF16)
        psT = [m.ps(f"q_psT{s}", [P, 512]) for s in range(2)]
        psQ = [[m.ps(f"q_ps{z}{s}", [P, 512]) for s in range(2)] for z in range(2)]
        psV = [m.ps(f"q_psV{s}", [P, 512]) for s in range(2)]
        s_xn, s_tp, s_xT, s_qk, s_v = (m.sem(n) for n in ("q_xn", "q_tp", "q_xT", "q_qk", "q_v"))
        s_f, s_vc, s_part = (m.sem(n) for n in ("q_sf", "q_vc", "q_spart"))
        s_out = [m.sem(f"q_out{s}") for s in range(2)]
        block = ctx.enter_context(nc.Block())

        @block.vector
        def _(dve):
            def norm(i, s, first):
                if not first:
                    dve.wait_ge(s_tp, 2 * i + s - 1)
                normalise_group(nc, g, xnb, i, s).then_inc(s_xn, 1)

            def split(i, s, first):
                dve.wait_ge(s_f, 4 * i + 2 * s + 2)
                if not first:
                    dve.wait_ge(s_out[s], i * 32)
                for z in range(2):
                    nc.vector.tensor_copy(part[:, s, z, 0, :], f[:, s, z, :])
                dve.drain()
                for z in range(2):
                    nc.vector.tensor_tensor(f[:, s, z, :], f[:, s, z, :], part[:, s, z, 0, :], ALU.subtract)
                dve.drain()
                for z in range(2):
                    nc.vector.tensor_copy(part[:, s, z, 1, :], f[:, s, z, :])
                dve.drain()
                for z in range(2):
                    nc.vector.tensor_tensor(part[:, s, z, 2, :], f[:, s, z, :], part[:, s, z, 1, :],
                                            ALU.subtract).then_inc(s_part, 1)

            norm(0, 0, True)
            norm(0, 1, True)
            for s in range(2):
                norm(1, s, False)
                split(0, s, True)
            with dve.Fori(1, B - 1) as i:
                for s in range(2):
                    norm(i + 1, s, False)
                    split(i, s, False)
            for s in range(2):
                split(B - 1, s, False)

        @block.tensor
        def _(pe):
            def group(i, s, first):
                pe.wait_ge(s_xn, 2 * i + s + 1)
                if not first:
                    pe.wait_ge(s_xT, 2 * i + s - 1)
                for j in range(4):
                    last = nc.tensor.transpose(psT[s][:, j * D:(j + 1) * D], xnb[:, s, j, :], g.ident)
                last.then_inc(s_tp, 1)
                pe.wait_ge(s_xT, 2 * i + s + 1)
                if not first:
                    pe.wait_ge(s_f, 4 * i + 2 * s - 2)
                    pe.wait_ge(s_vc, 2 * i + s - 1)
                for z in range(2):
                    nc.tensor.matmul(psQ[z][s][:], g.wqkv[:, z * D:(z + 1) * D], xT[:, s, :],
                                     start=True, stop=True).then_inc(s_qk, 1)
                for j in range(4):
                    last = nc.tensor.matmul(psV[s][:, j * D:(j + 1) * D], xT[:, s, j * D:(j + 1) * D],
                                            g.wqkv[:, 2 * D:3 * D], start=True, stop=True)
                last.then_inc(s_v, 1)

            for s in range(2):
                group(0, s, True)
            with pe.Fori(1, B) as i:
                for s in range(2):
                    group(i, s, False)

        @block.scalar
        def _(act):
            def group(i, s, first):
                act.wait_ge(s_tp, 2 * i + s + 1)
                if not first:
                    act.wait_ge(s_v, 2 * i + s - 1)
                nc.scalar.copy(xT[:, s, :], psT[s][:]).then_inc(s_xT, 1)
                for z in range(2):
                    act.wait_ge(s_qk, 4 * i + 2 * s + z + 1)
                    if not first:
                        act.wait_ge(s_part, 4 * i + 2 * s - 2 + z)
                    nc.scalar.activation(f[:, s, z, :], psQ[z][s][:], ACT.Copy,
                                         scale=(float(DH) ** -0.5 if z == 0 else 1.0)).then_inc(s_f, 1)
                act.wait_ge(s_v, 2 * i + s + 1)
                nc.scalar.copy(
                    g.v[:, bass.ds(i * HEADS, HEADS), s * 4:s * 4 + 4, :],
                    psV[s][:].rearrange("p (j h e) -> p h j e", j=4, h=HEADS)).then_inc(s_vc, 1)

            for s in range(2):
                group(0, s, True)
            with act.Fori(1, B) as i:
                for s in range(2):
                    group(i, s, False)

        @block.sync
        def _(sp):
            with sp.Fori(0, B) as i:
                for s in range(2):
                    for z in range(2):
                        sp.wait_ge(s_part, 4 * i + 2 * s + z + 1)
                        sp.dma_start(
                            d.qk[z, :, bass.ds(i * P, P), s * 512:(s + 1) * 512].rearrange("a p t -> p a t"),
                            part[:, s, z, :, :]).then_inc(s_out[s], 16)
            for s in range(2):
                sp.wait_ge(s_out[s], B * 32)


def phase_attention(nc, d, g):
    with ExitStack() as ctx:
        m = Mem(nc, ctx)
        qop = [m.sb(f"qop{n}", [TROWS, L], BF16) for n in range(NBUF)]
        kop = [m.sb(f"kop{n}", [TROWS, L], BF16) for n in range(NBUF)]
        prob = [m.sb(f"prob{s}", [P, KT * PBLK]) for s in range(2)]
        vst = [m.sb(f"vst{s}", [P, KT, VW]) for s in range(2)]
        nmax = [m.sb(f"nmax{s}", [P, KT]) for s in range(2)]
        res = m.sb("res", [P, KT])
        none = m.sb("none", [P, KT])
        mpart = [m.sb(f"mpart{s}", [P, 3, KT], BF16) for s in range(2)]
        mrow = [m.sb(f"mrow{s}", [3 * KT, P], BF16) for s in range(2)]
        identb = m.sb("identb", [P, P], BF16)
        osum = [m.sb(f"osum{s}", [P, HALF]) for s in range(2)]
        psS = [m.ps(f"psS{s}", [P, 2, HALF]) for s in range(2)]
        psE = [m.ps(f"psE{s}", [P, HALF]) for s in range(2)]
        psV = m.ps("psV", [P, HALF])
        psM = m.ps("psM", [P, HALF])
        psMb = psM[0:3 * KT, 0:P // 2].bitcast(BF16)
        s_op = [m.sem(f"s_op{n}") for n in range(NBUF)]
        s_mr = [m.sem(f"s_mr{n}") for n in range(NBUF)]
        s_init, s_one = m.sem("s_init"), m.sem("s_one")
        s_s, s_max = m.sem("s_s"), m.sem("s_max")
        s_mp, s_mt, s_mc = m.sem("s_mp"), m.sem("s_mt"), m.sem("s_mc")
        s_t, s_exp = m.sem("s_t"), m.sem("s_exp")
        s_diag, s_vst = m.sem("s_diag"), m.sem("s_vst")
        s_pv, s_ev, s_ot, s_oc = m.sem("s_pv"), m.sem("s_ev"), m.sem("s_ot"), m.sem("s_oc")
        block = ctx.enter_context(nc.Block())
        N = NHEAD

        def steps(eng, step, lo, hi):
            for i in range(lo, NBUF):
                step(i, i, i, 0)
            with eng.Fori(0, N // NBUF - 2) as q:
                for k in range(NBUF, 2 * NBUF):
                    step(q * NBUF + k, k, None, q)
            for i in range(N - NBUF, hi):
                step(i, i, i, 0)

        def live(at, head):
            return at is None or 0 <= at + head < N

        def later(at, head, n):
            return at is None or at + head >= n


        def filled(q, r, head):
            return q + (r + head) // NBUF + 1

        @block.sync
        def _(sp):
            for n in range(NBUF):
                sp.dma_start(qop[n][BIAS0:MAX0, :], d.qbias).then_inc(s_init, 16)
                sp.dma_start(kop[n][BIAS0:TROWS, :], d.kbias).then_inc(s_init, 16)

            def step(i, r, at, q):
                if live(at, 3):
                    b = (r + 3) % NBUF
                    if later(at, 3, NBUF):
                        sp.wait_ge(s_t, 16 * i)
                    for a in range(3):
                        rows = slice(a * 3 * DH, (a + 1) * 3 * DH)
                        src = d.qk[0, a, bass.ds((i + 3) * DH, DH), :]
                        sp.dma_start(qop[b][rows, :],
                                     src.unsqueeze(0).to_broadcast([3, DH, L])).then_inc(s_op[b], 16)
                        sp.dma_start(kop[b][rows, :],
                                     d.qk[1, :, bass.ds((i + 3) * DH, DH), :]).then_inc(s_op[b], 16)
                if live(at, 1):
                    b = (r + 1) % NBUF
                    sp.wait_ge(s_mc, i + 2)
                    sp.dma_start(qop[b][MAX0:TROWS, :].rearrange("a (t q) -> a t q", q=P),
                                 mrow[(r + 1) % 2][:]).then_inc(s_mr[b], 16)
            steps(sp, step, -3, 63)

        @block.tensor
        def _(pe):
            pe.wait_ge(s_init, 16 * 2 * NBUF)
            pe.wait_ge(s_one, 4)

            def step(i, r, at, q):
                for kt in range(KT):
                    if live(at, 0):
                        b = r % NBUF
                        if kt == 0:
                            pe.wait_ge(s_mr[b], 16 * filled(q, r, 0))
                        for half in range(2):
                            n = 2 * kt + half
                            if later(at, 0, 1) or n >= 2:
                                pe.wait_ge(s_exp, 16 * i + n - 1)
                            nc.tensor.matmul(psE[half][:], kop[b][0:TROWS, kt * P:(kt + 1) * P],
                                             qop[b][0:TROWS, half * HALF:(half + 1) * HALF],
                                             start=True, stop=True).then_inc(s_t, 1)
                    if live(at, 2):
                        b = (r + 2) % NBUF
                        if kt == 0:
                            pe.wait_ge(s_op[b], 96 * filled(q, r, 2))
                        if later(at, 2, 1) or kt >= 2:
                            pe.wait_ge(s_max, 8 * (i + 2) + kt - 1)
                        for half in range(2):
                            last = nc.tensor.matmul(psS[kt % 2][:, half, :],
                                                    qop[b][0:SROWS, kt * P:(kt + 1) * P],
                                                    kop[b][0:SROWS, half * HALF:(half + 1) * HALF],
                                                    start=True, stop=True)
                        last.then_inc(s_s, 1)
                    if kt == 2 and live(at, 1):
                        pe.wait_ge(s_mp, i + 2)
                        if later(at, -2, 1):
                            pe.wait_ge(s_oc, i - 2)
                        nc.tensor.transpose(psMb, mpart[(r + 1) % 2][:].rearrange("p a t -> p (a t)"),
                                            identb[:]).then_inc(s_mt, 1)
                    if kt == 5 and live(at, -2):
                        pe.wait_ge(s_ev, i - 1)
                        if live(at, 1):
                            pe.wait_ge(s_mc, i + 2)
                        elif later(at, -2, 1):
                            pe.wait_ge(s_oc, i - 2)
                        for c in range(4):
                            last = nc.tensor.matmul(psM[:, 64 + c * 2 * VW:64 + (c + 1) * 2 * VW],
                                                    osum[r % 2][:, c * P:(c + 1) * P],
                                                    g.const[:, C_SEL:C_SEL + 2 * VW], start=True, stop=True)
                        last.then_inc(s_ot, 1)
                    if kt % 2 == 1 and live(at, -1):
                        if kt == 1:
                            pe.wait_ge(s_vst, i)
                            if later(at, -1, 1):
                                pe.wait_ge(s_ev, i - 1)
                        if kt in (1, 5):
                            pe.wait_ge(s_diag, 2 * i - 1 + kt // 4)
                            pe.wait_ge(s_exp, 16 * i - 8 + 8 * (kt // 4))
                        for j in range(4):
                            k, half = kt - 1 + j // 2, j % 2
                            last = nc.tensor.matmul(
                                psV[32 * j:32 * j + VW, :], vst[(r + 1) % 2][:, k, :],
                                prob[(r + 1) % 2][:, k * PBLK + half * HALF:k * PBLK + (half + 1) * HALF],
                                start=(kt == 1), stop=(kt == 7))
                        if kt == 7:
                            last.then_inc(s_pv, 1)

            steps(pe, step, -2, 66)

        @block.vector
        def _(dve):
            nc.vector.memset(psV[:], 0.0).then_inc(s_one, 1)
            for s in range(2):
                nc.vector.memset(vst[s][:, :, DH:VW], 1.0).then_inc(s_one, 1)
            nc.vector.tensor_copy(identb[:], g.ident).then_inc(s_one, 1)

            def step(i, r, at, q):
                if live(at, 2):
                    for qt in range(KT):
                        dve.wait_ge(s_s, 8 * (i + 2) + qt + 1)
                        if qt == 0 and later(at, 2, 2):
                            dve.wait_ge(s_mp, i + 1)
                        nc.vector.tensor_reduce(nmax[r % 2][:, qt:qt + 1], psS[qt % 2][:], AX.XY, ALU.max,
                                                negate=True).then_inc(s_max, 1)
            steps(dve, step, -2, 62)

        @block.scalar
        def _(act):
            def step(i, r, at, q):
                if live(at, -2):
                    act.wait_ge(s_pv, i - 1)
                    if later(at, -2, 2):
                        act.wait_ge(s_ot, i - 3)
                    nc.scalar.copy(osum[r % 2][:], psV[:]).then_inc(s_ev, 1)
                for n in range(16):
                    if live(at, 0):
                        act.wait_ge(s_t, 16 * i + n + 1)
                        if n == 0 and later(at, 0, 2):
                            act.wait_ge(s_pv, i - 1)
                        kt, half = n // 2, n % 2
                        lo = kt * PBLK + half * HALF
                        nc.scalar.activation(prob[r % 2][:, lo:lo + HALF], psE[half][:],
                                             ACT.Exp).then_inc(s_exp, 1)
                    if n == 5 and live(at, 1):
                        act.wait_ge(s_mt, i + 2)
                        if later(at, 1, 2):
                            act.wait_ge(s_mr[(r + 3) % NBUF], 16 * filled(q, r, -1))
                        nc.scalar.copy(mrow[(r + 1) % 2][:], psMb).then_inc(s_mc, 1)
                    if n == 12 and live(at, -2):
                        act.wait_ge(s_ot, i - 1)
                        nc.scalar.copy(
                            g.att[:, bass.ds((i - 2) * KT * VW, KT * VW)].rearrange("p (f c e) -> p c f e",
                                                                                   f=2, c=4),
                            psM[:, 64:64 + 8 * VW].rearrange("p (c f e) -> p c f e", c=4, f=2)
                        ).then_inc(s_oc, 1)

            steps(act, step, -1, 66)

        @block.gpsimd
        def _(pool):
            pool.wait_ge(s_one, 4)
            nc.gpsimd.memset(none[:], 0.0)
            pool.drain()
            diag = g.const[:, C_DIAG:C_DIAG + KT * P].rearrange("p (k q) -> p k q", q=P)

            def step(i, r, at, q):
                if live(at, 1):
                    mp, nm = mpart[(r + 1) % 2], nmax[(r + 1) % 2]
                    pool.wait_ge(s_max, 8 * (i + 2))
                    if later(at, 1, 2):
                        pool.wait_ge(s_mt, i)
                    if later(at, 0, 2):
                        pool.wait_ge(s_pv, i - 1)
                    nc.gpsimd.tensor_tensor(mp[:, 0, :], nm[:], none[:], ALU.add)
                    pool.drain()
                    nc.gpsimd.tensor_tensor(res[:], nm[:], mp[:, 0, :], ALU.subtract)
                    pool.drain()
                    nc.gpsimd.tensor_copy(mp[:, 1, :], res[:])
                    pool.drain()
                    nc.gpsimd.tensor_tensor(mp[:, 2, :], res[:], mp[:, 1, :], ALU.subtract).then_inc(s_mp, 1)
                if live(at, 0):
                    if not live(at, 1):
                        pool.wait_ge(s_pv, i - 1)
                    nc.gpsimd.tensor_copy(
                        vst[r % 2][:, :, 0:DH].unsqueeze(1),
                        g.v[:, bass.ds(i, 1), :, :]).then_inc(s_vst, 1)
                    for h in range(2):
                        pool.wait_ge(s_exp, 16 * i + 8 * (h + 1))
                        dst = diag_blocks(prob[r % 2], h)
                        nc.gpsimd.tensor_tensor(dst, dst, diag[:, 4 * h:4 * h + 4, :],
                                                ALU.mult).then_inc(s_diag, 1)

            def diag_blocks(pr, h):
                full = pr[:, 0:P]
                return bass.AP(tensor=full.tensor, offset=4 * h * (PBLK + P),
                               ap=[list(full.ap[0]), [PBLK + P, 4], [1, P]])
            steps(pool, step, -1, 64)


def phase_project(nc, g):
    with ExitStack() as ctx:
        m = Mem(nc, ctx)
        rec = m.sb("rec", [P, 2, HEADS, 4])
        an = m.sb("an", [P, 2, 4, D])
        aT = m.sb("aT", [P, 2, 512])
        o = m.sb("o", [P, 2, 4, D])
        psT = [m.ps(f"p_psT{s}", [P, 512]) for s in range(2)]
        psO = [m.ps(f"p_psO{s}", [P, 512]) for s in range(2)]
        s_an, s_tp, s_aT, s_o, s_or = (m.sem(n) for n in ("p_an", "p_tp", "p_aT", "p_o", "p_or"))
        block = ctx.enter_context(nc.Block())
        att = g.att[:].rearrange("p (n t e) -> p n t e", t=KT, e=VW)

        @block.vector
        def _(dve):
            def norm(i, s, first):
                a = att[:, bass.ds(i * HEADS, HEADS), 4 * s:4 * s + 4, :]
                if not first:
                    dve.wait_ge(s_tp, 2 * i + s - 1)
                nc.vector.reciprocal(rec[:, s], a[:, :, :, DH])
                dve.drain()
                nc.vector.tensor_tensor(
                    an[:, s].rearrange("p j (h e) -> p h j e", e=DH), a[:, :, :, 0:DH],
                    rec[:, s].unsqueeze(3).to_broadcast([P, HEADS, 4, DH]), ALU.mult).then_inc(s_an, 1)

            def add(i, s):
                dve.wait_ge(s_o, 2 * i + s + 1)
                nc.vector.tensor_tensor(o[:, s], psO[s][:].rearrange("p (j d) -> p j d", d=D),
                                        g.bproj[:].unsqueeze(1).to_broadcast([P, 4, D]),
                                        ALU.add).then_inc(s_or, 1)
                dve.drain()
                at = bass.ds(i * 1024 + s * 512, 512)
                nc.vector.tensor_tensor(g.x[:, at], g.x[:, at], o[:, s].rearrange("p j d -> p (j d)"), ALU.add)

            norm(0, 0, True)
            norm(0, 1, True)
            with dve.Fori(0, B - 1) as i:
                for s in range(2):
                    norm(i + 1, s, False)
                    add(i, s)
            for s in range(2):
                add(B - 1, s)

        @block.tensor
        def _(pe):
            def group(i, s, first):
                pe.wait_ge(s_an, 2 * i + s + 1)
                if not first:
                    pe.wait_ge(s_aT, 2 * i + s - 1)
                for j in range(4):
                    last = nc.tensor.transpose(psT[s][:, j * D:(j + 1) * D], an[:, s, j, :], g.ident)
                last.then_inc(s_tp, 1)
                pe.wait_ge(s_aT, 2 * i + s + 1)
                if not first:
                    pe.wait_ge(s_or, 2 * i + s - 1)
                for j in range(4):
                    last = nc.tensor.matmul(psO[s][:, j * D:(j + 1) * D], aT[:, s, j * D:(j + 1) * D],
                                            g.wproj[:], start=True, stop=True)
                last.then_inc(s_o, 1)

            for s in range(2):
                group(0, s, True)
            with pe.Fori(1, B) as i:
                for s in range(2):
                    group(i, s, False)

        @block.scalar
        def _(act):
            def group(i, s, first):
                act.wait_ge(s_tp, 2 * i + s + 1)
                if not first:
                    act.wait_ge(s_o, 2 * i + s - 1)
                nc.scalar.copy(aT[:, s, :], psT[s][:]).then_inc(s_aT, 1)

            for s in range(2):
                group(0, s, True)
            with act.Fori(1, B) as i:
                for s in range(2):
                    group(i, s, False)


class Names:
    pass


def build(nc, ins, out):
    d, g = Names(), Names()
    d.x, d.w_qkv, d.w_proj, d.b_proj, d.router_w, d.router_b = ins[0:6]
    d.w1, d.b1, d.w2, d.b2, d.const, d.qbias, d.kbias = ins[6:13]
    d.sorted = nc.dram_tensor("sorted_tokens", (ET * P, D), F32, kind="Internal").ap()
    d.ysorted = nc.dram_tensor("sorted_results", (ET * P, D), F32, kind="Internal").ap()
    d.qk = nc.dram_tensor("qk_parts", (2, 3, NHEAD * DH, L), BF16, kind="Internal").ap()
    with ExitStack() as ctx:
        m = Mem(nc, ctx)
        g.x = m.sb("x", [P, NT * D])
        g.xn = m.sb("xn", [P, NT * D])
        g.const = m.sb("const", [P, C_END])
        g.ident = g.const[:, C_ID:C_ID + P]
        g.wr = m.sb("wr", [P, E])
        g.br = m.sb("br", [P, E])
        g.wqkv = m.sb("wqkv", [P, 3 * D])
        g.wproj = m.sb("wproj", [P, D])
        g.bproj = m.sb("bproj", [P, D])
        g.mean, g.var, g.std, g.rstd = (m.sb(n, [P, NT]) for n in ("mean", "var", "std", "rstd"))
        g.logit = m.sb("logit", [P, NT * E])
        g.pos = m.sb("pos", [P, NT], I32)
        g.eid = m.sb("eid", [1, ET], I32)
        phase_load(nc, d, g)

        def half_moe(tag, result):
            phase_norm_stats(nc, g, tag)
            phase_router(nc, g, tag)
            phase_route(nc, g, tag)
            phase_scatter(nc, d, g, tag)
            phase_experts(nc, d, g, tag)
            phase_gather(nc, d, g, tag, result)

        half_moe("a", None)
        phase_norm_stats(nc, g, "q")
        with ExitStack() as actx:
            am = Mem(nc, actx)
            g.v = am.sb("v", [P, NHEAD, KT, DH])
            g.att = am.sb("att", [P, NHEAD * KT * VW])
            phase_qkv(nc, d, g)
            phase_attention(nc, d, g)
            phase_project(nc, g)
        half_moe("b", out)


def kernel(L0_attn_x, L0_attn_w_qkv, L0_attn_w_proj, L0_attn_b_proj, L0_ffn_router_w, L0_ffn_router_b,
           L0_ffn_w1, L0_ffn_b1, L0_ffn_w2, L0_ffn_b2):
    import numpy as np
    import ml_dtypes
    import concourse.bacc as bacc
    from concourse.bass_utils import run_bass_kernel_spmd

    bf16 = ml_dtypes.bfloat16
    phi = np.float32((1.0 + np.sqrt(5.0)) / 2.0)
    pos = (np.arange(L, dtype=np.float32) * phi) % np.float32(1.0)
    order = np.argsort(pos, kind="stable")
    p = pos[order]

    def parts(a):
        hi = a.astype(bf16)
        mid = (a - hi.astype(np.float32)).astype(bf16)
        lo = (a - hi.astype(np.float32) - mid.astype(np.float32)).astype(bf16)
        return hi, mid, lo

    tile = np.arange(L) // P
    qbias = np.zeros((6, KT, L), bf16)
    kbias = np.zeros((6 * KT + 3, L), bf16)
    for t in range(KT):
        sign = np.where(tile <= t, np.float32(1), np.float32(-1))
        for a, part in enumerate(parts(p)):
            qbias[a, t] = (sign * part.astype(np.float32)).astype(bf16)
            qbias[3 + a, t] = (-sign).astype(bf16)
            kbias[a * KT + t] = (tile == t).astype(bf16)
            kbias[(3 + a) * KT + t] = np.where(tile == t, part.astype(np.float32), np.float32(0)).astype(bf16)
    kbias[6 * KT:] = np.ones((3, L), bf16)

    const = np.zeros((P, C_END), np.float32)
    const[:, C_ID:C_ID + P] = np.eye(P)
    const[:, C_TRI:C_TRI + P] = np.triu(np.ones((P, P)), 1)
    const[:, C_ONE:C_ONE + P] = 1.0
    for j in range(4):
        for e in range(VW):
            const[32 * j + e, C_SEL + (j % 2) * VW + e] = 1.0
    for t in range(KT):
        pt = p[t * P:(t + 1) * P].astype(np.float64)
        const[:, C_DIAG + t * P:C_DIAG + (t + 1) * P] = np.exp(-2.0 * np.maximum(0.0, pt[None, :] - pt[:, None]))
    const[:, C_IOTA:C_IOTA + E] = np.arange(E) - E
    const[:, C_TILE:C_TILE + ET] = np.arange(ET) * P

    def tiled(a):
        return np.ascontiguousarray(a.reshape(NT, P, D).transpose(1, 0, 2)).reshape(P, NT * D)

    arrays = {
        "x": tiled(np.asarray(L0_attn_x)[:, order, :]),
        "w_qkv": np.asarray(L0_attn_w_qkv), "w_proj": np.asarray(L0_attn_w_proj),
        "b_proj": np.asarray(L0_attn_b_proj),
        "router_w": np.asarray(L0_ffn_router_w), "router_b": np.asarray(L0_ffn_router_b),
        "w1": np.ascontiguousarray(np.asarray(L0_ffn_w1).transpose(1, 0, 2)).reshape(P, E * 2 * HID),
        "b1": np.asarray(L0_ffn_b1).reshape(E * 2 * HID),
        "w2": np.ascontiguousarray(np.asarray(L0_ffn_w2).reshape(E, HID // P, P, D).transpose(2, 0, 1, 3))
                .reshape(P, E * HID),
        "b2": np.asarray(L0_ffn_b2).reshape(E * D),
        "const": const, "qbias": qbias.reshape(6 * KT, L), "kbias": kbias,
    }
    arrays = {f"in_{n}": np.ascontiguousarray(a) for n, a in arrays.items()}
    nc = bacc.Bacc("TRN2", target_bir_lowering=False, num_devices=1)
    ins = [nc.dram_tensor(n, a.shape, mybir.dt.from_np(a.dtype), kind="ExternalInput").ap()
           for n, a in arrays.items()]
    out = nc.dram_tensor("out_x", (P, NT * D), F32, kind="ExternalOutput").ap()
    build(nc, ins, out)
    r = run_bass_kernel_spmd(nc, [arrays], core_ids=[0])
    y = np.asarray(r.results[0]["out_x"]).reshape(P, NT, D).transpose(1, 0, 2).reshape(B, L, D)
    back = np.empty_like(order)
    back[order] = np.arange(L)
    return y[:, back, :]
```

```python
from contextlib import ExitStack

import concourse.bass as bass
from concourse import mybir

P = 128
D = 128
B, L = 4, 1024
NTOK = B * L
NT = NTOK // P
HEADS, DH = 16, 8
NHEAD = B * HEADS
E, HID = 8, 512
ET = NT + E
KT = L // P
HALF = 512
VW = DH + 1
COMBO = 9 * DH
BIAS0, BIASN = COMBO, 6 * KT
MAX0 = BIAS0 + BIASN
SROWS = MAX0
TROWS = MAX0 + 3
PBLK = L + P
XBUF = 4
NBUF = 4
LN_EPS = 1e-5

ALU = mybir.AluOpType
ACT = mybir.ActivationFunctionType
AX = mybir.AxisListType
F32 = mybir.dt.float32
BF16 = mybir.dt.bfloat16
I32 = mybir.dt.int32

C_ID, C_TRI, C_ONE, C_SEL, C_DIAG, C_IOTA, C_TILE, C_END = 0, 128, 256, 384, 512, 1536, 1544, 1584


class Mem:

    def __init__(self, nc, ctx):
        self.nc, self.ctx = nc, ctx

    def sb(self, name, shape, dt=F32):
        return self.ctx.enter_context(self.nc.sbuf_tensor(name, shape, dt))

    def ps(self, name, shape, dt=F32):
        return self.ctx.enter_context(self.nc.psum_tensor(name, shape, dt))

    def sem(self, name):
        return self.ctx.enter_context(self.nc.semaphore(name))


def load_experts(sp, d, g):
    sp.dma_start(g.w1[:], d.w1).then_inc(g.s_w, 16)
    sp.dma_start(g.w2[:], d.w2).then_inc(g.s_w, 16)
    sp.dma_start(g.b1[:], d.b1.partition_broadcast(P)).then_inc(g.s_w, 16)
    sp.dma_start(g.b2[:], d.b2.partition_broadcast(P)).then_inc(g.s_w, 16)


def phase_load(nc, d, g):
    with ExitStack() as ctx:
        m = Mem(nc, ctx)
        zero = m.sb("zero", [P, D])
        s_loaded, s_zero, s_cleared = m.sem("s_loaded"), m.sem("s_zero"), m.sem("s_cleared")
        block = ctx.enter_context(nc.Block())

        @block.sync
        def _(sp):
            sp.dma_start(g.x[:], d.x).then_inc(s_loaded, 16)
            sp.dma_start(g.const[:], d.const).then_inc(s_loaded, 16)
            sp.dma_start(g.wr[:], d.router_w).then_inc(s_loaded, 16)
            sp.dma_start(g.br[:], d.router_b.partition_broadcast(P)).then_inc(s_loaded, 16)
            load_experts(sp, d, g)
            sp.dma_start(g.wqkv[:], d.w_qkv).then_inc(s_loaded, 16)
            sp.dma_start(g.wproj[:], d.w_proj).then_inc(s_loaded, 16)
            sp.dma_start(g.bproj[:], d.b_proj.partition_broadcast(P)).then_inc(s_loaded, 16)
            sp.wait_ge(s_zero, 1)
            sp.dma_start(d.sorted.rearrange("(t p) d -> p t d", p=P),
                         zero[:].unsqueeze(1).to_broadcast([P, ET, D])).then_inc(s_cleared, 16)
            sp.wait_ge(s_loaded, 7 * 16)
            sp.wait_ge(s_cleared, 16)

        @block.gpsimd
        def _(pool):
            nc.gpsimd.memset(zero[:], 0.0).then_inc(s_zero, 1)


def phase_norm_stats(nc, g, tag):
    with ExitStack() as ctx:
        m = Mem(nc, ctx)
        stats = m.sb(f"stats{tag}", [P, 4, 6])
        mv = m.sb(f"mv{tag}", [P, 4, 2])
        s_var, s_std = m.sem(f"s_var{tag}"), m.sem(f"s_std{tag}")
        block = ctx.enter_context(nc.Block())

        @block.vector
        def _(dve):
            with dve.Fori(0, NT // 4) as i:
                for j in range(4):
                    nc.vector.bn_stats(stats[:, j, :], g.x[:, bass.ds(i * 512 + j * D, D)])
                dve.drain()
                for j in range(4):
                    nc.vector.bn_aggr(mv[:, j, :], stats[:, j, :])
                dve.drain()
                nc.vector.tensor_copy(g.mean[:, bass.ds(i * 4, 4)], mv[:, :, 0])
                nc.vector.tensor_scalar(g.var[:, bass.ds(i * 4, 4)], mv[:, :, 1], LN_EPS, None, ALU.add)
                dve.drain()
            dve.drain().then_inc(s_var, 1)
            dve.wait_ge(s_std, 1)
            nc.vector.reciprocal(g.rstd[:], g.std[:])

        @block.scalar
        def _(act):
            act.wait_ge(s_var, 1)
            nc.scalar.activation(g.std[:], g.var[:], ACT.Sqrt).then_inc(s_std, 1)


def normalise_group(nc, g, out, i, s):
    for j in range(4):
        last = nc.vector.tensor_scalar(
            out[:, s, j, :], g.x[:, bass.ds(i * 1024 + s * 512 + j * D, D)],
            g.mean[:, bass.ds(i * 8 + s * 4 + j, 1)], g.rstd[:, bass.ds(i * 8 + s * 4 + j, 1)],
            ALU.subtract, ALU.mult)
    return last


def phase_router(nc, g, tag):
    with ExitStack() as ctx:
        m = Mem(nc, ctx)
        xnb = m.sb(f"xnb{tag}", [P, 2, 4, D])
        xT = m.sb(f"xT{tag}", [P, 2, 512])
        psT = [m.ps(f"psT{tag}{s}", [P, 512]) for s in range(2)]
        psL = [m.ps(f"psL{tag}{s}", [P, 512]) for s in range(2)]
        s_xn, s_tp, s_xT = m.sem(f"s_xn{tag}"), m.sem(f"s_tp{tag}"), m.sem(f"s_xT{tag}")
        s_kept, s_lp, s_lg = m.sem(f"s_kept{tag}"), m.sem(f"s_lp{tag}"), m.sem(f"s_lg{tag}")
        block = ctx.enter_context(nc.Block())

        @block.vector
        def _(dve):
            def norm(i, s, first):
                if not first:
                    dve.wait_ge(s_tp, 2 * i + s - 1)
                    dve.wait_ge(s_kept, 2 * i + s - 1)
                normalise_group(nc, g, xnb, i, s).then_inc(s_xn, 1)

            def logits(i, s):
                dve.wait_ge(s_lp, 2 * i + s + 1)
                nc.vector.tensor_tensor(
                    g.logit[:, bass.ds(i * 64 + s * 32, 32)].rearrange("p (j e) -> p j e", e=E),
                    psL[s][:, 0:32].rearrange("p (j e) -> p j e", e=E),
                    g.br[:].unsqueeze(1).to_broadcast([P, 4, E]), ALU.add).then_inc(s_lg, 1)

            norm(0, 0, True)
            norm(0, 1, True)
            with dve.Fori(0, B - 1) as i:
                for s in range(2):
                    norm(i + 1, s, False)
                    logits(i, s)
            for s in range(2):
                logits(B - 1, s)

        @block.tensor
        def _(pe):
            def group(i, s, first):
                pe.wait_ge(s_xn, 2 * i + s + 1)
                if not first:
                    pe.wait_ge(s_xT, 2 * i + s - 1)
                for j in range(4):
                    last = nc.tensor.transpose(psT[s][:, j * D:(j + 1) * D], xnb[:, s, j, :], g.ident)
                last.then_inc(s_tp, 1)
                pe.wait_ge(s_xT, 2 * i + s + 1)
                if not first:
                    pe.wait_ge(s_lg, 2 * i + s - 1)
                for j in range(4):
                    last = nc.tensor.matmul(psL[s][:, j * E:(j + 1) * E], xT[:, s, j * D:(j + 1) * D],
                                            g.wr[:], start=True, stop=True)
                last.then_inc(s_lp, 1)

            for s in range(2):
                group(0, s, True)
            with pe.Fori(1, B) as i:
                for s in range(2):
                    group(i, s, False)

        @block.scalar
        def _(act):
            def group(i, s, first):
                act.wait_ge(s_tp, 2 * i + s + 1)
                if not first:
                    act.wait_ge(s_lp, 2 * i + s - 1)
                nc.scalar.copy(xT[:, s, :], psT[s][:]).then_inc(s_xT, 1)
                nc.scalar.copy(g.xn[:, bass.ds(i * 1024 + s * 512, 512)],
                               xnb[:, s, :, :].rearrange("p j d -> p (j d)")).then_inc(s_kept, 1)

            for s in range(2):
                group(0, s, True)
            with act.Fori(1, B) as i:
                for s in range(2):
                    group(i, s, False)


def phase_route(nc, g, tag):
    with ExitStack() as ctx:
        m = Mem(nc, ctx)
        N = NT * E
        best = m.sb(f"best{tag}", [P, NT])
        eq = m.sb(f"eq{tag}", [P, NT, E])
        pick = m.sb(f"pick{tag}", [P, NT])
        hot = m.sb(f"hot{tag}", [P, E, NT])
        total = m.sb(f"total{tag}", [P, E, NT])
        incl = m.sb(f"incl{tag}", [P, E, NT])
        excl = m.sb(f"excl{tag}", [P, E, NT])
        ones = m.sb(f"ones{tag}", [P, N])
        row = m.sb(f"row{tag}", [P, E, NT])
        cnt = m.sb(f"cnt{tag}", [P, E])
        whole = m.sb(f"whole{tag}", [P, E], I32)
        pad = m.sb(f"pad{tag}", [P, E])
        end = m.sb(f"end{tag}", [P, E])
        off = m.sb(f"off{tag}", [P, E])
        posf = m.sb(f"posf{tag}", [P, NT])
        before = m.sb(f"before{tag}", [1, ET, E])
        eidf = m.sb(f"eidf{tag}", [1, ET])
        psR = m.ps(f"psR{tag}", [P, 512])
        psC = m.ps(f"psC{tag}", [P, 512])
        s_hot, s_rank = m.sem(f"s_hot{tag}"), m.sem(f"s_rank{tag}")
        block = ctx.enter_context(nc.Block())
        iota = g.const[:, C_IOTA:C_IOTA + E]
        lg = g.logit[:].rearrange("p (t e) -> p t e", e=E)

        @block.vector
        def _(dve):
            nc.vector.memset(ones[:], 1.0)
            nc.vector.tensor_reduce(best[:], lg, AX.X, ALU.max)
            dve.drain()
            nc.vector.tensor_tensor(eq[:], lg, best[:].unsqueeze(2).to_broadcast([P, NT, E]), ALU.is_equal)
            dve.drain()
            nc.vector.tensor_tensor(eq[:], eq[:], iota.unsqueeze(1).to_broadcast([P, NT, E]), ALU.mult)
            dve.drain()
            nc.vector.tensor_reduce(pick[:], eq[:], AX.X, ALU.min)
            dve.drain()
            nc.vector.tensor_tensor(hot[:].rearrange("p e t -> p t e"),
                                    iota.unsqueeze(1).to_broadcast([P, NT, E]),
                                    pick[:].unsqueeze(2).to_broadcast([P, NT, E]),
                                    ALU.is_equal).then_inc(s_hot, 1)
            dve.wait_ge(s_rank, 1)
            nc.vector.tensor_copy(total[:].rearrange("p e t -> p (e t)"), psC[:, 0:N])
            dve.drain()
            nc.vector.tensor_tensor_scan(incl[:].rearrange("p e t -> p (e t)"), ones[:],
                                         total[:].rearrange("p e t -> p (e t)"), 0.0, ALU.mult, ALU.add)
            dve.drain()
            nc.vector.tensor_tensor(excl[:], incl[:], total[:], ALU.subtract)
            dve.drain()
            nc.vector.tensor_tensor(cnt[:], incl[:, :, NT - 1], excl[:, :, 0], ALU.subtract)
            nc.vector.tensor_tensor(row[:].rearrange("p e t -> p (e t)"), psR[:, 0:N],
                                    excl[:].rearrange("p e t -> p (e t)"), ALU.add)
            dve.drain()
            nc.vector.tensor_scalar(pad[:], cnt[:], float(P - 1), None, ALU.add)
            dve.drain()
            nc.vector.tensor_copy(whole[:], pad[:])
            dve.drain()
            nc.vector.tensor_scalar(whole[:], whole[:], 7, 7, ALU.logical_shift_right,
                                    ALU.logical_shift_left)
            dve.drain()
            nc.vector.tensor_copy(pad[:], whole[:])
            dve.drain()
            nc.vector.tensor_tensor_scan(end[:], ones[:, 0:E], pad[:], 0.0, ALU.mult, ALU.add)
            dve.drain()
            nc.vector.tensor_tensor(off[:], end[:], pad[:], ALU.subtract)
            dve.drain()
            nc.vector.tensor_tensor(off[:], off[:], excl[:, :, 0], ALU.subtract)
            nc.vector.tensor_tensor(before[:], end[0:1, :].unsqueeze(1).to_broadcast([1, ET, E]),
                                    g.const[0:1, C_TILE:C_TILE + ET].unsqueeze(2).to_broadcast([1, ET, E]),
                                    ALU.is_le)
            dve.drain()
            nc.vector.tensor_tensor(row[:], row[:], off[:].unsqueeze(2).to_broadcast([P, E, NT]), ALU.add)
            nc.vector.tensor_reduce(eidf[:], before[:], AX.X, ALU.add)
            dve.drain()
            nc.vector.tensor_tensor(row[:], row[:], hot[:], ALU.mult)
            nc.vector.tensor_scalar(g.eid[:], eidf[:], float(E - 1), None, ALU.min)
            dve.drain()
            nc.vector.tensor_reduce(posf[:], row[:].rearrange("p e t -> p t e"), AX.X, ALU.add)
            dve.drain()
            nc.vector.tensor_copy(g.pos[:], posf[:])

        @block.tensor
        def _(pe):
            pe.wait_ge(s_hot, 1)
            flat = hot[:].rearrange("p e t -> p (e t)")
            nc.tensor.matmul(psR[:, 0:N], g.const[:, C_TRI:C_TRI + P], flat, start=True, stop=True)
            nc.tensor.matmul(psC[:, 0:N], g.const[:, C_ONE:C_ONE + P], flat, start=True,
                             stop=True).then_inc(s_rank, 1)


def phase_scatter(nc, d, g, tag):
    with ExitStack() as ctx:
        m = Mem(nc, ctx)
        s_put = m.sem(f"s_put{tag}")
        block = ctx.enter_context(nc.Block())

        @block.gpsimd
        def _(pool):
            for t in range(NT):
                pool.indirect_dma_start(
                    out=d.sorted, out_offset=bass.IndirectOffsetOnAxis(ap=g.pos[:, t:t + 1], axis=0),
                    in_=g.xn[:, t * D:(t + 1) * D], in_offset=None).then_inc(s_put, 16)
            pool.wait_ge(s_put, 16 * NT)


def phase_experts(nc, d, g, tag):
    with ExitStack() as ctx:
        m = Mem(nc, ctx)
        w1, w2, b1, b2 = g.w1, g.w2, g.b1, g.b2
        xs = m.sb(f"xs{tag}", [P, XBUF, D])
        xsT = m.sb(f"xsT{tag}", [P, 2, P])
        gate = m.sb(f"gate{tag}", [P, 2, HID])
        sig = m.sb(f"sig{tag}", [P, 2, HID])
        up = m.sb(f"up{tag}", [P, 2, HID])
        hid = m.sb(f"hid{tag}", [P, 2, HID])
        hidT = m.sb(f"hidT{tag}", [P, 2, HID])
        y = m.sb(f"y{tag}", [P, 2, D])
        psA = [m.ps(f"psA{tag}{s}", [P, HID]) for s in range(2)]
        psG = [m.ps(f"psG{tag}{s}", [P, HID]) for s in range(2)]
        psX = m.ps(f"psX{tag}", [P, 512])
        psH = m.ps(f"psH{tag}", [P, 512])
        psY = m.ps(f"psY{tag}", [P, 512])
        S = {n: m.sem(f"s_{n}{tag}") for n in
             ("xt", "xsT", "h", "gate", "sig", "up", "hid", "ht", "hidT", "yp", "y")}
        s_xs = [m.sem(f"s_xs{tag}{n}") for n in range(XBUF)]
        s_st = [m.sem(f"s_st{tag}{s}") for s in range(2)]
        block = ctx.enter_context(nc.Block())
        T = ET

        def steps(eng, step):
            for i in range(1 - XBUF, XBUF):
                step(i, i, i, 0)
            with eng.Fori(0, T // XBUF - 2) as q:
                for r in range(XBUF, 2 * XBUF):
                    step(q * XBUF + r, r, None, q)
            for i in range(T - XBUF, T + 2):
                step(i, i, i, 0)

        def live(at, lag):
            return at is None or 0 <= at - lag < T

        def later(at, lag, n):
            return at is None or at - lag >= n

        @block.sync
        def _(sp):
            def step(i, r, at, q):
                if live(at, -3):
                    if later(at, -3, XBUF):
                        sp.wait_ge(S["xt"], i)
                    n = (r + 3) % XBUF
                    sp.dma_start(xs[:, n, :], d.sorted[bass.ds((i + 3) * P, P), :]).then_inc(s_xs[n], 16)
                if live(at, 2):
                    sp.wait_ge(S["y"], i - 1)
                    sp.dma_start(d.ysorted[bass.ds((i - 2) * P, P), :], y[:, r % 2, :])\
                        .then_inc(s_st[r % 2], 16)
            steps(sp, step)
            for s in range(2):
                sp.wait_ge(s_st[s], 16 * (T // 2))

        @block.tensor
        def _(pe):
            pe.wait_ge(g.s_w, 64)
            def expert(i):
                return pe.value_load(g.eid[0:1, bass.ds(i, 1)], min_val=0, max_val=E - 1)

            def step(i, r, at, q):
                s = r % 2
                if live(at, -1):
                    pe.wait_ge(s_xs[(r + 1) % XBUF], 16 * (q + (r + 1) // XBUF + 1))
                    if later(at, -1, 1):
                        pe.wait_ge(S["xsT"], i + 1)
                    nc.tensor.transpose(psX[:, 0:P], xs[:, (r + 1) % XBUF, :], g.ident).then_inc(S["xt"], 1)
                if live(at, 0):
                    e = expert(i)
                    pe.wait_ge(S["xsT"], i + 1)
                    if later(at, 0, 2):
                        pe.wait_ge(S["up"], i - 1)
                    nc.tensor.matmul(psG[s][:], xsT[:, s, :], w1[:, bass.ds(e * 2 * HID + HID, HID)],
                                     start=True, stop=True).then_inc(S["h"], 1)
                    nc.tensor.matmul(psA[s][:], xsT[:, s, :], w1[:, bass.ds(e * 2 * HID, HID)],
                                     start=True, stop=True).then_inc(S["h"], 1)
                if live(at, 1):
                    pe.wait_ge(S["hid"], i)
                    if later(at, 1, 1):
                        pe.wait_ge(S["hidT"], i - 1)
                    for c in range(4):
                        last = nc.tensor.transpose(psH[:, c * P:(c + 1) * P],
                                                   hid[:, 1 - s, c * P:(c + 1) * P], g.ident)
                    last.then_inc(S["ht"], 1)
                if live(at, 2):
                    e = expert(i - 2)
                    pe.wait_ge(S["hidT"], i - 1)
                    if later(at, 2, 1):
                        pe.wait_ge(S["y"], i - 2)
                    for c in range(4):
                        last = nc.tensor.matmul(psY[:, 0:D], hidT[:, s, c * P:(c + 1) * P],
                                                w2[:, bass.ds(e * HID + c * P, P)],
                                                start=(c == 0), stop=(c == 3))
                    last.then_inc(S["yp"], 1)
            steps(pe, step)

        @block.vector
        def _(dve):
            dve.wait_ge(g.s_w, 64)

            def expert(i):
                return dve.value_load(g.eid[0:1, bass.ds(i, 1)], min_val=0, max_val=E - 1)

            def step(i, r, at, q):
                s = r % 2
                if live(at, 0):
                    e = expert(i)
                    dve.wait_ge(S["h"], 2 * i + 1)
                    if later(at, 0, 2):
                        dve.wait_ge(S["sig"], i - 1)
                    nc.vector.tensor_tensor(gate[:, s, :], psG[s][:], b1[:, bass.ds(e * 2 * HID + HID, HID)],
                                            ALU.add).then_inc(S["gate"], 1)
                    dve.wait_ge(S["h"], 2 * i + 2)
                    nc.vector.tensor_tensor(up[:, s, :], psA[s][:], b1[:, bass.ds(e * 2 * HID, HID)],
                                            ALU.add).then_inc(S["up"], 1)
                if live(at, 2):
                    e = expert(i - 2)
                    dve.wait_ge(S["yp"], i - 1)
                    if later(at, 2, 2):
                        dve.wait_ge(s_st[s], 16 * (2 * q + r // 2 - 1))
                    nc.vector.tensor_tensor(y[:, s, :], psY[:, 0:D], b2[:, bass.ds(e * D, D)],
                                            ALU.add).then_inc(S["y"], 1)
                if live(at, 0):
                    dve.wait_ge(S["sig"], i + 1)
                    dve.wait_ge(S["up"], i + 1)
                    if later(at, 0, 2):
                        dve.wait_ge(S["ht"], i - 1)
                    nc.vector.tensor_tensor(hid[:, s, :], up[:, s, :], sig[:, s, :],
                                            ALU.mult).then_inc(S["hid"], 1)
            steps(dve, step)

        @block.scalar
        def _(act):
            def step(i, r, at, q):
                s = r % 2
                if live(at, -1):
                    act.wait_ge(S["xt"], i + 2)
                    if later(at, -1, 2):
                        act.wait_ge(S["h"], 2 * i)
                    nc.scalar.copy(xsT[:, 1 - s, :], psX[:, 0:P]).then_inc(S["xsT"], 1)
                if live(at, 1):
                    act.wait_ge(S["ht"], i)
                    if later(at, 1, 2):
                        act.wait_ge(S["yp"], i - 2)
                    nc.scalar.copy(hidT[:, 1 - s, :], psH[:]).then_inc(S["hidT"], 1)
                if live(at, 0):
                    act.wait_ge(S["gate"], i + 1)
                    if later(at, 0, 2):
                        act.wait_ge(S["hid"], i - 1)
                    nc.scalar.activation(sig[:, s, :], gate[:, s, :], ACT.Sigmoid).then_inc(S["sig"], 1)
            steps(act, step)


def phase_gather(nc, d, g, tag, out):
    with ExitStack() as ctx:
        m = Mem(nc, ctx)
        s_got = [m.sem(f"s_got{tag}{n}") for n in range(NT // 4)]
        s_add, s_out = m.sem(f"s_add{tag}"), m.sem(f"s_out{tag}")
        block = ctx.enter_context(nc.Block())

        @block.gpsimd
        def _(pool):
            for t in range(NT):
                pool.indirect_dma_start(
                    out=g.xn[:, t * D:(t + 1) * D], out_offset=None, in_=d.ysorted,
                    in_offset=bass.IndirectOffsetOnAxis(ap=g.pos[:, t:t + 1], axis=0))\
                    .then_inc(s_got[t // 4], 16)

        @block.vector
        def _(dve):
            for n in range(NT // 4):
                dve.wait_ge(s_got[n], 64)
                at = slice(n * 512, (n + 1) * 512)
                nc.vector.scalar_tensor_tensor(out=g.x[:, at], in0=g.xn[:, at], scalar=0.5,
                                               in1=g.x[:, at], op0=ALU.mult, op1=ALU.add)\
                    .then_inc(s_add, 1)

        if out is not None:
            @block.sync
            def _(sp):
                with sp.Fori(0, NT // 4) as i:
                    sp.wait_ge(s_add, i + 1)
                    at = bass.ds(i * 512, 512)
                    sp.dma_start(out[:, at], g.x[:, at]).then_inc(s_out, 16)
                sp.wait_ge(s_out, 16 * (NT // 4))


def phase_qkv(nc, d, g):
    with ExitStack() as ctx:
        m = Mem(nc, ctx)
        xnb = m.sb("q_xnb", [P, 2, 4, D])
        xT = m.sb("q_xT", [P, 2, 512])
        f = m.sb("q_f", [P, 2, 2, 512])
        part = m.sb("q_part", [P, 2, 2, 3, 512], BF16)
        psT = [m.ps(f"q_psT{s}", [P, 512]) for s in range(2)]
        psQ = [[m.ps(f"q_ps{z}{s}", [P, 512]) for s in range(2)] for z in range(2)]
        psV = [m.ps(f"q_psV{s}", [P, 512]) for s in range(2)]
        s_xn, s_tp, s_xT, s_qk, s_v = (m.sem(n) for n in ("q_xn", "q_tp", "q_xT", "q_qk", "q_v"))
        s_f, s_vc, s_part = (m.sem(n) for n in ("q_sf", "q_vc", "q_spart"))
        s_out = [m.sem(f"q_out{s}") for s in range(2)]
        block = ctx.enter_context(nc.Block())

        @block.vector
        def _(dve):
            def norm(i, s, first):
                if not first:
                    dve.wait_ge(s_tp, 2 * i + s - 1)
                normalise_group(nc, g, xnb, i, s).then_inc(s_xn, 1)

            def split(i, s, first):
                dve.wait_ge(s_f, 4 * i + 2 * s + 2)
                if not first:
                    dve.wait_ge(s_out[s], i * 32)
                for z in range(2):
                    nc.vector.tensor_copy(part[:, s, z, 0, :], f[:, s, z, :])
                dve.drain()
                for z in range(2):
                    nc.vector.tensor_tensor(f[:, s, z, :], f[:, s, z, :], part[:, s, z, 0, :], ALU.subtract)
                dve.drain()
                for z in range(2):
                    nc.vector.tensor_copy(part[:, s, z, 1, :], f[:, s, z, :])
                dve.drain()
                for z in range(2):
                    nc.vector.tensor_tensor(part[:, s, z, 2, :], f[:, s, z, :], part[:, s, z, 1, :],
                                            ALU.subtract).then_inc(s_part, 1)

            norm(0, 0, True)
            norm(0, 1, True)
            for s in range(2):
                norm(1, s, False)
                split(0, s, True)
            with dve.Fori(1, B - 1) as i:
                for s in range(2):
                    norm(i + 1, s, False)
                    split(i, s, False)
            for s in range(2):
                split(B - 1, s, False)

        @block.tensor
        def _(pe):
            def group(i, s, first):
                pe.wait_ge(s_xn, 2 * i + s + 1)
                if not first:
                    pe.wait_ge(s_xT, 2 * i + s - 1)
                for j in range(4):
                    last = nc.tensor.transpose(psT[s][:, j * D:(j + 1) * D], xnb[:, s, j, :], g.ident)
                last.then_inc(s_tp, 1)
                pe.wait_ge(s_xT, 2 * i + s + 1)
                if not first:
                    pe.wait_ge(s_f, 4 * i + 2 * s - 2)
                    pe.wait_ge(s_vc, 2 * i + s - 1)
                for z in range(2):
                    nc.tensor.matmul(psQ[z][s][:], g.wqkv[:, z * D:(z + 1) * D], xT[:, s, :],
                                     start=True, stop=True).then_inc(s_qk, 1)
                for j in range(4):
                    last = nc.tensor.matmul(psV[s][:, j * D:(j + 1) * D], xT[:, s, j * D:(j + 1) * D],
                                            g.wqkv[:, 2 * D:3 * D], start=True, stop=True)
                last.then_inc(s_v, 1)

            for s in range(2):
                group(0, s, True)
            with pe.Fori(1, B) as i:
                for s in range(2):
                    group(i, s, False)

        @block.scalar
        def _(act):
            def group(i, s, first):
                act.wait_ge(s_tp, 2 * i + s + 1)
                if not first:
                    act.wait_ge(s_v, 2 * i + s - 1)
                nc.scalar.copy(xT[:, s, :], psT[s][:]).then_inc(s_xT, 1)
                for z in range(2):
                    act.wait_ge(s_qk, 4 * i + 2 * s + z + 1)
                    if not first:
                        act.wait_ge(s_part, 4 * i + 2 * s - 2 + z)
                    nc.scalar.activation(f[:, s, z, :], psQ[z][s][:], ACT.Copy,
                                         scale=(float(DH) ** -0.5 if z == 0 else 1.0)).then_inc(s_f, 1)
                act.wait_ge(s_v, 2 * i + s + 1)
                nc.scalar.copy(
                    g.v[:, bass.ds(i * HEADS, HEADS), s * 4:s * 4 + 4, :],
                    psV[s][:].rearrange("p (j h e) -> p h j e", j=4, h=HEADS)).then_inc(s_vc, 1)

            for s in range(2):
                group(0, s, True)
            with act.Fori(1, B) as i:
                for s in range(2):
                    group(i, s, False)

        @block.sync
        def _(sp):
            with sp.Fori(0, B) as i:
                for s in range(2):
                    for z in range(2):
                        sp.wait_ge(s_part, 4 * i + 2 * s + z + 1)
                        sp.dma_start(
                            d.qk[z, :, bass.ds(i * P, P), s * 512:(s + 1) * 512].rearrange("a p t -> p a t"),
                            part[:, s, z, :, :]).then_inc(s_out[s], 16)
            for s in range(2):
                sp.wait_ge(s_out[s], B * 32)


def phase_attention(nc, d, g):
    with ExitStack() as ctx:
        m = Mem(nc, ctx)
        qop = [m.sb(f"qop{n}", [TROWS, L], BF16) for n in range(NBUF)]
        kop = [m.sb(f"kop{n}", [TROWS, L], BF16) for n in range(NBUF)]
        prob = [m.sb(f"prob{s}", [P, KT * PBLK]) for s in range(2)]
        vst = [m.sb(f"vst{s}", [P, KT, VW]) for s in range(2)]
        nmax = [m.sb(f"nmax{s}", [P, KT]) for s in range(2)]
        res = m.sb("res", [P, KT])
        none = m.sb("none", [P, KT])
        mpart = [m.sb(f"mpart{s}", [P, 3, KT], BF16) for s in range(2)]
        mrow = [m.sb(f"mrow{s}", [3 * KT, P], BF16) for s in range(2)]
        identb = m.sb("identb", [P, P], BF16)
        osum = [m.sb(f"osum{s}", [P, HALF]) for s in range(2)]
        psS = [m.ps(f"psS{s}", [P, 2, HALF]) for s in range(2)]
        psE = [m.ps(f"psE{s}", [P, HALF]) for s in range(2)]
        psV = m.ps("psV", [P, HALF])
        psM = m.ps("psM", [P, HALF])
        psMb = psM[0:3 * KT, 0:P // 2].bitcast(BF16)
        s_op = [m.sem(f"s_op{n}") for n in range(NBUF)]
        s_mr = [m.sem(f"s_mr{n}") for n in range(NBUF)]
        s_init, s_one = m.sem("s_init"), m.sem("s_one")
        s_s, s_max = m.sem("s_s"), m.sem("s_max")
        s_mp, s_mt, s_mc = m.sem("s_mp"), m.sem("s_mt"), m.sem("s_mc")
        s_t, s_exp = m.sem("s_t"), m.sem("s_exp")
        s_diag, s_vst = m.sem("s_diag"), m.sem("s_vst")
        s_pv, s_ev = m.sem("s_pv"), m.sem("s_ev")
        s_os = [m.sem(f"s_os{s}") for s in range(2)]
        block = ctx.enter_context(nc.Block())
        N = NHEAD

        def steps(eng, step, lo, hi):
            for i in range(lo, NBUF):
                step(i, i, i, 0)
            with eng.Fori(0, N // NBUF - 2) as q:
                for k in range(NBUF, 2 * NBUF):
                    step(q * NBUF + k, k, None, q)
            for i in range(N - NBUF, hi):
                step(i, i, i, 0)

        def live(at, head):
            return at is None or 0 <= at + head < N

        def later(at, head, n):
            return at is None or at + head >= n


        def filled(q, r, head):
            return q + (r + head) // NBUF + 1

        @block.sync
        def _(sp):
            for n in range(NBUF):
                sp.dma_start(qop[n][BIAS0:MAX0, :], d.qbias).then_inc(s_init, 16)
                sp.dma_start(kop[n][BIAS0:TROWS, :], d.kbias).then_inc(s_init, 16)

            def step(i, r, at, q):
                if live(at, 3):
                    b = (r + 3) % NBUF
                    if later(at, 3, NBUF):
                        sp.wait_ge(s_t, 16 * i)
                    for a in range(3):
                        rows = slice(a * 3 * DH, (a + 1) * 3 * DH)
                        src = d.qk[0, a, bass.ds((i + 3) * DH, DH), :]
                        sp.dma_start(qop[b][rows, :],
                                     src.unsqueeze(0).to_broadcast([3, DH, L])).then_inc(s_op[b], 16)
                        sp.dma_start(kop[b][rows, :],
                                     d.qk[1, :, bass.ds((i + 3) * DH, DH), :]).then_inc(s_op[b], 16)
                if live(at, -2):
                    sp.wait_ge(s_ev, i - 1)
                    for j in range(4):
                        sp.dma_start(d.sums[bass.ds(i - 2, 1), j // 2, :,
                                            (j % 2) * HALF:(j % 2 + 1) * HALF].squeeze(),
                                     osum[r % 2][32 * j:32 * j + VW, :]).then_inc(s_os[r % 2], 16)
                if live(at, 1):
                    b = (r + 1) % NBUF
                    sp.wait_ge(s_mc, i + 2)
                    sp.dma_start(qop[b][MAX0:TROWS, :].rearrange("a (t q) -> a t q", q=P),
                                 mrow[(r + 1) % 2][:]).then_inc(s_mr[b], 16)
            steps(sp, step, -3, N + 2)
            for s in range(2):
                sp.wait_ge(s_os[s], 64 * (N // 2))

        @block.tensor
        def _(pe):
            pe.wait_ge(s_init, 16 * 2 * NBUF)
            pe.wait_ge(s_one, 4)

            def step(i, r, at, q):
                for kt in range(KT):
                    for half in range(2):
                        cols = slice(half * HALF, (half + 1) * HALF)
                        if live(at, 0):
                            b, n = r % NBUF, 2 * kt + half
                            if n == 0:
                                pe.wait_ge(s_mr[b], 16 * filled(q, r, 0))
                            if later(at, 0, 1) or n >= 2:
                                pe.wait_ge(s_exp, 16 * i + n - 1)
                            nc.tensor.matmul(psE[half][:], kop[b][0:TROWS, kt * P:(kt + 1) * P],
                                             qop[b][0:TROWS, cols], start=True, stop=True).then_inc(s_t, 1)
                        if live(at, 2):
                            b = (r + 2) % NBUF
                            if kt == 0 and half == 0:
                                pe.wait_ge(s_op[b], 96 * filled(q, r, 2))
                            if half == 0 and (later(at, 2, 1) or kt >= 2):
                                pe.wait_ge(s_max, 8 * (i + 2) + kt - 1)
                            last = nc.tensor.matmul(psS[kt % 2][:, half, :],
                                                    qop[b][0:SROWS, kt * P:(kt + 1) * P],
                                                    kop[b][0:SROWS, cols], start=True, stop=True)
                            if half == 1:
                                last.then_inc(s_s, 1)
                    if kt == 2 and live(at, 1):
                        pe.wait_ge(s_mp, i + 2)
                        if later(at, 1, 1):
                            pe.wait_ge(s_mc, i + 1)
                        nc.tensor.transpose(psMb, mpart[(r + 1) % 2][:].rearrange("p a t -> p (a t)"),
                                            identb[:]).then_inc(s_mt, 1)
                    if kt % 2 == 1 and live(at, -1):
                        if kt == 1:
                            pe.wait_ge(s_vst, i)
                            if later(at, -1, 1):
                                pe.wait_ge(s_ev, i - 1)
                        if kt in (1, 5):
                            pe.wait_ge(s_diag, 2 * i - 1 + kt // 4)
                            pe.wait_ge(s_exp, 16 * i - 8 + 8 * (kt // 4))
                        for j in range(4):
                            k, half = kt - 1 + j // 2, j % 2
                            last = nc.tensor.matmul(
                                psV[32 * j:32 * j + VW, :], vst[(r + 1) % 2][:, k, :],
                                prob[(r + 1) % 2][:, k * PBLK + half * HALF:k * PBLK + (half + 1) * HALF],
                                start=(kt == 1), stop=(kt == 7))
                        if kt == 7:
                            last.then_inc(s_pv, 1)

            steps(pe, step, -2, N + 1)

        @block.vector
        def _(dve):
            nc.vector.memset(psV[:], 0.0).then_inc(s_one, 1)
            for s in range(2):
                nc.vector.memset(vst[s][:, :, DH:VW], 1.0).then_inc(s_one, 1)
            nc.vector.tensor_copy(identb[:], g.ident).then_inc(s_one, 1)

            def step(i, r, at, q):
                if live(at, 2):
                    for qt in range(KT):
                        dve.wait_ge(s_s, 8 * (i + 2) + qt + 1)
                        if qt == 0 and later(at, 2, 2):
                            dve.wait_ge(s_mp, i + 1)
                        nc.vector.tensor_reduce(nmax[r % 2][:, qt:qt + 1], psS[qt % 2][:], AX.XY, ALU.max,
                                                negate=True).then_inc(s_max, 1)
            steps(dve, step, -2, 62)

        @block.scalar
        def _(act):
            def step(i, r, at, q):
                if live(at, -2):
                    act.wait_ge(s_pv, i - 1)
                    if later(at, -2, 2):
                        act.wait_ge(s_os[r % 2], 64 * (2 * q + r // 2 - 1))
                    nc.scalar.copy(osum[r % 2][:], psV[:]).then_inc(s_ev, 1)
                for n in range(16):
                    if live(at, 0):
                        act.wait_ge(s_t, 16 * i + n + 1)
                        if n == 0 and later(at, 0, 2):
                            act.wait_ge(s_pv, i - 1)
                        kt, half = n // 2, n % 2
                        lo = kt * PBLK + half * HALF
                        nc.scalar.activation(prob[r % 2][:, lo:lo + HALF], psE[half][:],
                                             ACT.Exp).then_inc(s_exp, 1)
                    if n == 5 and live(at, 1):
                        act.wait_ge(s_mt, i + 2)
                        if later(at, 1, 2):
                            act.wait_ge(s_mr[(r + 3) % NBUF], 16 * filled(q, r, -1))
                        nc.scalar.copy(mrow[(r + 1) % 2][:], psMb).then_inc(s_mc, 1)
            steps(act, step, -1, 66)

        @block.gpsimd
        def _(pool):
            pool.wait_ge(s_one, 4)
            nc.gpsimd.memset(none[:], 0.0)
            pool.drain()
            diag = g.const[:, C_DIAG:C_DIAG + KT * P].rearrange("p (k q) -> p k q", q=P)

            def step(i, r, at, q):
                if live(at, 1):
                    mp, nm = mpart[(r + 1) % 2], nmax[(r + 1) % 2]
                    pool.wait_ge(s_max, 8 * (i + 2))
                    if later(at, 1, 2):
                        pool.wait_ge(s_mt, i)
                    if later(at, 0, 2):
                        pool.wait_ge(s_pv, i - 1)
                    nc.gpsimd.tensor_tensor(mp[:, 0, :], nm[:], none[:], ALU.add)
                    pool.drain()
                    nc.gpsimd.tensor_tensor(res[:], nm[:], mp[:, 0, :], ALU.subtract)
                    pool.drain()
                    nc.gpsimd.tensor_copy(mp[:, 1, :], res[:])
                    pool.drain()
                    nc.gpsimd.tensor_tensor(mp[:, 2, :], res[:], mp[:, 1, :], ALU.subtract).then_inc(s_mp, 1)
                if live(at, 0):
                    if not live(at, 1):
                        pool.wait_ge(s_pv, i - 1)
                    nc.gpsimd.tensor_copy(
                        vst[r % 2][:, :, 0:DH].unsqueeze(1),
                        g.v[:, bass.ds(i, 1), :, :]).then_inc(s_vst, 1)
                    for h in range(2):
                        pool.wait_ge(s_exp, 16 * i + 8 * (h + 1))
                        dst = diag_blocks(prob[r % 2], h)
                        nc.gpsimd.tensor_tensor(dst, dst, diag[:, 4 * h:4 * h + 4, :],
                                                ALU.mult).then_inc(s_diag, 1)

            def diag_blocks(pr, h):
                full = pr[:, 0:P]
                return bass.AP(tensor=full.tensor, offset=4 * h * (PBLK + P),
                               ap=[list(full.ap[0]), [PBLK + P, 4], [1, P]])
            steps(pool, step, -1, 64)


def phase_project(nc, d, g):
    with ExitStack() as ctx:
        m = Mem(nc, ctx)
        num = m.sb("num", [P, B, 2, L])
        den = m.sb("den", [HEADS, B, 2, L])
        xb = m.sb("xb", [P, 2, 4, D])
        rec = m.sb("rec", [HEADS, 2, HALF])
        aT = m.sb("aT", [P, 2, HALF])
        psD = [m.ps(f"p_psD{s}", [P, HALF]) for s in range(2)]
        psO = [m.ps(f"p_psO{s}", [P, HALF]) for s in range(2)]
        s_ld = [m.sem(f"p_ld{b}") for b in range(B)]
        s_num, s_xb, s_rec, s_exp, s_aT, s_o, s_or = (
            m.sem(n) for n in ("p_num", "p_xb", "p_rec", "p_exp", "p_aT", "p_o", "p_or"))
        block = ctx.enter_context(nc.Block())
        steps = [(b, s) for b in range(B) for s in range(2)]
        sums = d.sums.rearrange("(b h) a e t -> b a h e t", h=HEADS)

        @block.sync
        def _(sp):
            for b in range(B):
                for a in range(2):
                    sp.dma_start(num[:, b, a, :], sums[b, a, :, 0:DH, :]).then_inc(s_ld[b], 16)
                    sp.dma_start(den[:, b, a, :], sums[b, a, :, DH, :]).then_inc(s_ld[b], 16)
            load_experts(sp, d, g)

        @block.gpsimd
        def _(pool):
            for n, (b, s) in enumerate(steps):
                cols = slice(s * HALF, (s + 1) * HALF)
                if n >= 2:
                    pool.wait_ge(s_or, n - 1)
                x = g.x[:, n * HALF:(n + 1) * HALF].rearrange("p (j d) -> p j d", d=D)
                nc.gpsimd.tensor_tensor(xb[:, s], x, g.bproj[:].unsqueeze(1).to_broadcast([P, 4, D]),
                                        ALU.add).then_inc(s_xb, 1)
                pool.wait_ge(s_ld[b], 64)
                nc.gpsimd.tensor_tensor(num[:, b, 0, cols], num[:, b, 0, cols], num[:, b, 1, cols],
                                        ALU.add).then_inc(s_num, 1)

        @block.vector
        def _(dve):
            def reciprocals(n):
                b, s = steps[n]
                cols = slice(s * HALF, (s + 1) * HALF)
                dve.wait_ge(s_ld[b], 64)
                nc.vector.tensor_tensor(den[:, b, 0, cols], den[:, b, 0, cols], den[:, b, 1, cols], ALU.add)
                dve.drain()
                if n >= 2:
                    dve.wait_ge(s_exp, n - 1)
                nc.vector.reciprocal(rec[:, s, :], den[:, b, 0, cols]).then_inc(s_rec, 1)

            reciprocals(0)
            for n, (b, s) in enumerate(steps):
                if n + 1 < len(steps):
                    reciprocals(n + 1)
                dve.wait_ge(s_exp, n + 1)
                dve.wait_ge(s_num, n + 1)
                if n >= 2:
                    dve.wait_ge(s_o, n - 1)
                nc.vector.tensor_tensor(aT[:, s, :], num[:, b, 0, s * HALF:(s + 1) * HALF], psD[s][:],
                                        ALU.mult).then_inc(s_aT, 1)
                dve.wait_ge(s_o, n + 1)
                dve.wait_ge(s_xb, n + 1)
                nc.vector.tensor_tensor(g.x[:, n * HALF:(n + 1) * HALF], psO[s][:],
                                        xb[:, s].rearrange("p j d -> p (j d)"), ALU.add).then_inc(s_or, 1)

        @block.tensor
        def _(pe):
            for n, (b, s) in enumerate(steps):
                pe.wait_ge(s_rec, n + 1)
                if n >= 2:
                    pe.wait_ge(s_aT, n - 1)
                nc.tensor.matmul(psD[s][:], g.const[0:HEADS, C_SEL:C_SEL + P], rec[:, s, :],
                                 start=True, stop=True).then_inc(s_exp, 1)
                pe.wait_ge(s_aT, n + 1)
                if n >= 2:
                    pe.wait_ge(s_or, n - 1)
                for j in range(4):
                    last = nc.tensor.matmul(psO[s][:, j * D:(j + 1) * D], aT[:, s, j * D:(j + 1) * D],
                                            g.wproj[:], start=True, stop=True)
                last.then_inc(s_o, 1)


class Names:
    pass


def build(nc, ins, out):
    d, g = Names(), Names()
    d.x, d.w_qkv, d.w_proj, d.b_proj, d.router_w, d.router_b = ins[0:6]
    d.w1, d.b1, d.w2, d.b2, d.const, d.qbias, d.kbias = ins[6:13]
    d.sorted = nc.dram_tensor("sorted_tokens", (ET * P, D), F32, kind="Internal").ap()
    d.ysorted = nc.dram_tensor("sorted_results", (ET * P, D), F32, kind="Internal").ap()
    d.sums = nc.dram_tensor("weighted_sums", (NHEAD, 2, VW, L), F32, kind="Internal").ap()
    d.qk = nc.dram_tensor("qk_parts", (2, 3, NHEAD * DH, L), BF16, kind="Internal").ap()
    with ExitStack() as ctx:
        m = Mem(nc, ctx)
        g.x = m.sb("x", [P, NT * D])
        g.xn = m.sb("xn", [P, NT * D])
        g.const = m.sb("const", [P, C_END])
        g.ident = g.const[:, C_ID:C_ID + P]
        g.wr = m.sb("wr", [P, E])
        g.br = m.sb("br", [P, E])
        g.wqkv = m.sb("wqkv", [P, 3 * D])
        g.wproj = m.sb("wproj", [P, D])
        g.bproj = m.sb("bproj", [P, D])
        g.mean, g.var, g.std, g.rstd = (m.sb(n, [P, NT]) for n in ("mean", "var", "std", "rstd"))
        g.logit = m.sb("logit", [P, NT * E])
        g.pos = m.sb("pos", [P, NT], I32)
        g.eid = m.sb("eid", [1, ET], I32)

        def experts_memory(tag, ectx):
            em = Mem(nc, ectx)
            g.w1, g.w2 = em.sb(f"w1{tag}", [P, E * 2 * HID]), em.sb(f"w2{tag}", [P, E * HID])
            g.b1, g.b2 = em.sb(f"b1{tag}", [P, E * 2 * HID]), em.sb(f"b2{tag}", [P, E * D])
            g.s_w = em.sem(f"s_w{tag}")

        def half_moe(tag, result):
            phase_norm_stats(nc, g, tag)
            phase_router(nc, g, tag)
            phase_route(nc, g, tag)
            phase_scatter(nc, d, g, tag)
            phase_experts(nc, d, g, tag)
            phase_gather(nc, d, g, tag, result)

        with ExitStack() as ectx:
            experts_memory("a", ectx)
            phase_load(nc, d, g)
            half_moe("a", None)
        phase_norm_stats(nc, g, "q")
        with ExitStack() as actx:
            am = Mem(nc, actx)
            g.v = am.sb("v", [P, NHEAD, KT, DH])
            phase_qkv(nc, d, g)
            phase_attention(nc, d, g)
        with ExitStack() as ectx:
            experts_memory("b", ectx)
            phase_project(nc, d, g)
            half_moe("b", out)


def kernel(L0_attn_x, L0_attn_w_qkv, L0_attn_w_proj, L0_attn_b_proj, L0_ffn_router_w, L0_ffn_router_b,
           L0_ffn_w1, L0_ffn_b1, L0_ffn_w2, L0_ffn_b2):
    import numpy as np
    import ml_dtypes
    import concourse.bacc as bacc
    from concourse.bass_utils import run_bass_kernel_spmd

    bf16 = ml_dtypes.bfloat16
    phi = np.float32((1.0 + np.sqrt(5.0)) / 2.0)
    pos = (np.arange(L, dtype=np.float32) * phi) % np.float32(1.0)
    order = np.argsort(pos, kind="stable")
    p = pos[order]

    def parts(a):
        hi = a.astype(bf16)
        mid = (a - hi.astype(np.float32)).astype(bf16)
        lo = (a - hi.astype(np.float32) - mid.astype(np.float32)).astype(bf16)
        return hi, mid, lo

    tile = np.arange(L) // P
    qbias = np.zeros((6, KT, L), bf16)
    kbias = np.zeros((6 * KT + 3, L), bf16)
    for t in range(KT):
        sign = np.where(tile <= t, np.float32(1), np.float32(-1))
        for a, part in enumerate(parts(p)):
            qbias[a, t] = (sign * part.astype(np.float32)).astype(bf16)
            qbias[3 + a, t] = (-sign).astype(bf16)
            kbias[a * KT + t] = (tile == t).astype(bf16)
            kbias[(3 + a) * KT + t] = np.where(tile == t, part.astype(np.float32), np.float32(0)).astype(bf16)
    kbias[6 * KT:] = np.ones((3, L), bf16)

    const = np.zeros((P, C_END), np.float32)
    const[:, C_ID:C_ID + P] = np.eye(P)
    const[:, C_TRI:C_TRI + P] = np.triu(np.ones((P, P)), 1)
    const[:, C_ONE:C_ONE + P] = 1.0
    for h in range(HEADS):
        const[h, C_SEL + h * DH:C_SEL + (h + 1) * DH] = 1.0
    for t in range(KT):
        pt = p[t * P:(t + 1) * P].astype(np.float64)
        const[:, C_DIAG + t * P:C_DIAG + (t + 1) * P] = np.exp(-2.0 * np.maximum(0.0, pt[None, :] - pt[:, None]))
    const[:, C_IOTA:C_IOTA + E] = np.arange(E) - E
    const[:, C_TILE:C_TILE + ET] = np.arange(ET) * P

    def tiled(a):
        return np.ascontiguousarray(a.reshape(NT, P, D).transpose(1, 0, 2)).reshape(P, NT * D)

    arrays = {
        "x": tiled(np.asarray(L0_attn_x)[:, order, :]),
        "w_qkv": np.asarray(L0_attn_w_qkv), "w_proj": np.asarray(L0_attn_w_proj),
        "b_proj": np.asarray(L0_attn_b_proj),
        "router_w": np.asarray(L0_ffn_router_w), "router_b": np.asarray(L0_ffn_router_b),
        "w1": np.ascontiguousarray(np.asarray(L0_ffn_w1).transpose(1, 0, 2)).reshape(P, E * 2 * HID),
        "b1": np.asarray(L0_ffn_b1).reshape(E * 2 * HID),
        "w2": np.ascontiguousarray(np.asarray(L0_ffn_w2).reshape(E, HID // P, P, D).transpose(2, 0, 1, 3))
                .reshape(P, E * HID),
        "b2": np.asarray(L0_ffn_b2).reshape(E * D),
        "const": const, "qbias": qbias.reshape(6 * KT, L), "kbias": kbias,
    }
    arrays = {f"in_{n}": np.ascontiguousarray(a) for n, a in arrays.items()}
    nc = bacc.Bacc("TRN2", target_bir_lowering=False, num_devices=1)
    ins = [nc.dram_tensor(n, a.shape, mybir.dt.from_np(a.dtype), kind="ExternalInput").ap()
           for n, a in arrays.items()]
    out = nc.dram_tensor("out_x", (P, NT * D), F32, kind="ExternalOutput").ap()
    build(nc, ins, out)
    r = run_bass_kernel_spmd(nc, [arrays], core_ids=[0])
    y = np.asarray(r.results[0]["out_x"]).reshape(P, NT, D).transpose(1, 0, 2).reshape(B, L, D)
    back = np.empty_like(order)
    back[order] = np.arange(L)
    return y[:, back, :]
```

```python
from contextlib import ExitStack

import concourse.bass as bass
from concourse import mybir

P = 128
D = 128
B, L = 4, 1024
NTOK = B * L
NT = NTOK // P
HEADS, DH = 16, 8
NHEAD = B * HEADS
E, HID = 8, 512
ET = NT + E - 1
REGION = NTOK + P
SPARE = E - 1
ROW = {"a": D + 1, "b": 2 * D + 1}
W1 = 2 * HID + 2 * HID // P
KT = L // P
HALF = 512
VW = DH + 1
COMBO = 9 * DH
BIAS0, BIASN = COMBO, 6 * KT
MAX0 = BIAS0 + BIASN
SROWS = MAX0
TROWS = MAX0 + 3
PBLK = L + P
XBUF = 4
NBUF = 4
LN_EPS = 1e-5

ALU = mybir.AluOpType
ACT = mybir.ActivationFunctionType
AX = mybir.AxisListType
F32 = mybir.dt.float32
BF16 = mybir.dt.bfloat16
I32 = mybir.dt.int32

C_ID, C_TRI, C_ONE, C_IOTA, C_BASE, C_CARRY, C_TOK, C_TILE = 0, 128, 256, 384, 392, 400, 440, 472
C_DIAG = C_TILE + ET
C_END = C_DIAG + KT * P


class Mem:

    def __init__(self, nc, ctx):
        self.nc, self.ctx = nc, ctx

    def sb(self, name, shape, dt=F32):
        return self.ctx.enter_context(self.nc.sbuf_tensor(name, shape, dt))

    def ps(self, name, shape, dt=F32):
        return self.ctx.enter_context(self.nc.psum_tensor(name, shape, dt))

    def sem(self, name):
        return self.ctx.enter_context(self.nc.semaphore(name))


def scatter_group(nc, pool, d, g, xn, n):
    row = ROW[g.turn]
    for t in range(4 * n, 4 * n + 4):
        pool.indirect_dma_start(
            out=d.sorted[g.turn], out_offset=bass.IndirectOffsetOnAxis(ap=g.pos[:, t:t + 1], axis=0),
            in_=xn[:, t * row:(t + 1) * row], in_offset=None).then_inc(g.s_put, 16)


class Plan:

    def __init__(self, m, tag, counts):
        self.cnt, self.pad, self.end, self.step = (
            m.sb(f"{n}_{tag}", [1, E]) for n in ("cnt", "pad", "end", "step"))
        self.whole, self.padrow = m.sb(f"whole_{tag}", [1, E], I32), m.sb(f"padrow_{tag}", [1, E], I32)
        self.before = m.sb(f"before_{tag}", [1, ET, E])
        self.eidf, self.rows = m.sb(f"eidf_{tag}", [1, ET]), m.sb(f"rows_{tag}", [1, ET])
        self.s_cnt, self.s_padrow = m.sem(f"s_cnt_{tag}"), m.sem(f"s_padrow_{tag}")
        self.s_pad = [m.sem(f"s_pad{n}_{tag}") for n in range(2)]
        self.counts = counts


def plan_padding(eng, d, g, p, experts):
    done = p.s_pad[experts[0] != 0]
    eng.wait_ge(p.s_padrow, 1)
    for e in experts:
        r = eng.value_load(p.padrow[0:1, e:e + 1], min_val=e * REGION, max_val=e * REGION + NTOK)
        eng.dma_start(d.sorted[g.turn][bass.ds(r, P), :], d.padding[e * P:(e + 1) * P, 0:ROW[g.turn]])\
            .then_inc(done, 16)
    eng.wait_ge(done, 16 * len(experts))


def plan_tiles(nc, dve, g, p):
    tile_row = g.const[0:1, C_TILE:C_TILE + ET]
    dve.wait_ge(p.s_cnt, 1)
    nc.vector.tensor_copy(p.padrow[:], p.counts[0:1, 0:E]).then_inc(p.s_padrow, 1)
    nc.vector.tensor_tensor(p.cnt[:], p.counts[0:1, 0:E], g.const[0:1, C_BASE:C_BASE + E], ALU.subtract)
    dve.drain()
    nc.vector.tensor_scalar(p.pad[:], p.cnt[:], float(P - 1), None, ALU.add)
    dve.drain()
    nc.vector.tensor_copy(p.whole[:], p.pad[:])
    dve.drain()
    nc.vector.tensor_scalar(p.whole[:], p.whole[:], 7, 7, ALU.logical_shift_right,
                            ALU.logical_shift_left)
    dve.drain()
    nc.vector.tensor_copy(p.pad[:], p.whole[:])
    dve.drain()
    nc.vector.tensor_tensor_scan(p.end[:], g.const[0:1, C_ONE:C_ONE + E], p.pad[:], 0.0, ALU.mult, ALU.add)
    nc.vector.tensor_scalar(p.step[:], p.pad[:], -1.0, float(REGION), ALU.mult, ALU.add)
    dve.drain()
    nc.vector.tensor_tensor(p.before[:], p.end[:].unsqueeze(1).to_broadcast([1, ET, E]),
                            tile_row.unsqueeze(2).to_broadcast([1, ET, E]), ALU.is_le)
    dve.drain()
    nc.vector.tensor_reduce(p.eidf[:], p.before[:], AX.X, ALU.add)
    dve.drain()
    nc.vector.tensor_tensor(p.before[:], p.before[:], p.step[:].unsqueeze(1).to_broadcast([1, ET, E]),
                            ALU.mult)
    nc.vector.tensor_scalar(g.eid[:], p.eidf[:], float(E - 1), None, ALU.min)
    dve.drain()
    nc.vector.tensor_reduce(p.rows[:], p.before[:], AX.X, ALU.add)
    dve.drain()
    nc.vector.tensor_tensor(p.rows[:], p.rows[:], tile_row, ALU.add)
    dve.drain()
    nc.vector.tensor_copy(g.trow[:], p.rows[:])


def phase_tokens(nc, d, g, tag):
    groups = NT // 4
    first, attend, last_part = tag == "first", tag == "attend", tag == "last"
    with ExitStack() as ctx:
        m = Mem(nc, ctx)

        def sem(name):
            return m.sem(f"s_{name}_{tag}")

        def sb(name, shape, dt=F32):
            return m.sb(f"{name}_{tag}", shape, dt)

        def banks(name):
            return [m.ps(f"{name}{s}_{tag}", [P, HALF]) for s in range(2)]

        stats, mv = sb("stats", [P, 2, 4, 6]), sb("mv", [P, 2, 4, 2])
        var, std, rstd = (sb(n, [P, 2, 4]) for n in ("var", "std", "rstd"))
        xT = sb("xT", [P, 2, HALF])
        psT = banks("psT")
        s_var, s_std, s_xn, s_tp, s_xT, s_used = (
            sem(n) for n in ("var", "std", "xn", "tp", "xT", "used"))
        row_len = D if attend else ROW[g.turn]
        xn_rows = sb("xn", [P, NT * row_len])
        xn = xn_rows[:].rearrange("p (t r) -> p t r", r=row_len)
        xt = xn[:, :, D + 1:] if last_part else g.x[:].rearrange("p (t d) -> p t d", d=D)
        s_src = [sem(f"src{n}") for n in range(groups)]
        if attend:
            part = sb("part", [P, 2, 2, 3, HALF], BF16)
            rest = sb("rest", [P, 2, 2, HALF])
            psQ = [banks(f"psQ{z}") for z in range(2)]
            psV = banks("psV")
            s_new, s_qk, s_v, s_hi, s_rest, s_mid, s_part = (
                sem(n) for n in ("new", "qk", "v", "hi", "rest", "mid", "part"))
            yb = sb("yb", [P, NT * D])
            s_out = g.s_out
        else:
            psL = banks("psL")
            logit, eq, row = (sb(n, [P, 2, 4, E]) for n in ("logit", "eq", "row"))
            hot, upto = sb("hot", [P, 2, E, 5]), sb("upto", [P, 2, E, 5])
            best, pick, posf = (sb(n, [P, 2, 4]) for n in ("best", "pick", "posf"))
            s_upto, s_rank, s_read, s_pos = sem("upto"), sem("rank"), sem("read"), sem("pos")
            plan = Plan(m, tag, psL[groups % 2])
        if last_part:
            num, den, pickhead = g.num, g.den, g.pickhead
            s_num_in, s_den_in = g.s_num_in, g.s_den_in
            rec = sb("rec", [P, 2, P])
            aT = sb("aT", [P, 2, HALF])
            psD, psO = banks("psD"), banks("psO")
            s_num, s_rec, s_each, s_aT, s_o, s_x = (
                sem(n) for n in ("num", "rec", "each", "aT", "o", "x"))
        if first:
            s_small = sem("small")
        block = ctx.enter_context(nc.Block())
        scale = (float(DH) ** -0.5, 1.0)

        def cols(n):
            return slice(n * HALF, (n + 1) * HALF)

        def half(n):
            return n // 2, slice(n % 2 * HALF, (n % 2 + 1) * HALF)

        def live(n):
            return 0 <= n < groups

        @block.sync
        def _(sp):
            if first:
                sp.dma_start(g.const[:, 0:C_DIAG], d.const[:, 0:C_DIAG]).then_inc(s_small, 16)
                sp.dma_start(g.wr[:], d.router_w).then_inc(s_small, 16)
                sp.dma_start(g.br[:], d.router_b.partition_broadcast(P)).then_inc(s_small, 16)
                for n in range(groups):
                    sp.dma_start(g.x[:, cols(n)], d.x[:, cols(n)]).then_inc(s_src[n], 16)
                for turn in "ab":
                    sp.dma_start(d.sorted[turn][E * REGION:, :], d.padding[E * P:, 0:ROW[turn]])\
                        .then_inc(g.s_spare, 16)
                sp.dma_start(g.w1[:], d.w1).then_inc(g.s_w, 16)
                sp.dma_start(g.w2[:], d.w2).then_inc(g.s_w, 16)
                sp.dma_start(g.b2[:], d.b2.partition_broadcast(P)).then_inc(g.s_w, 16)
                sp.dma_start(g.const[:, C_DIAG:], d.const[:, C_DIAG:]).then_inc(g.s_later, 16)
                sp.dma_start(g.wqkv[:], d.w_qkv).then_inc(g.s_later, 16)
                sp.dma_start(g.wproj[:], d.w_proj).then_inc(g.s_later, 16)
                sp.dma_start(g.bproj[:], d.b_proj.partition_broadcast(P)).then_inc(g.s_later, 16)
                sp.wait_ge(g.s_spare, 32)
                sp.wait_ge(g.s_later, 64)
            if last_part:
                sp.dma_start(g.w1[:], d.w1).then_inc(g.s_w, 16)
                for s in range(2):
                    sp.wait_ge(g.s_os[s], 64 * (NHEAD // 2))
                for b in range(2, B):
                    sp.wait_ge(s_rec, b - 1)
                    sp.wait_ge(s_aT, 2 * b - 2)
                    load_sums(sp, d, g, b)
                sp.dma_start(g.w2[:], d.w2).then_inc(g.s_w, 16)
                sp.dma_start(g.b2[:], d.b2.partition_broadcast(P)).then_inc(g.s_w, 16)
            if attend:
                load_results(sp, d, yb, s_src)
                for n in range(NBUF):
                    sp.dma_start(g.qop[n][BIAS0:MAX0, :], d.qbias).then_inc(g.s_init, 16)
                    sp.dma_start(g.kop[n][BIAS0:TROWS, :], d.kbias).then_inc(g.s_init, 16)
                for n in range(groups):
                    b, c = half(n)
                    for z in range(2):
                        sp.wait_ge(s_part, 2 * n + z + 1)
                        sp.dma_start(d.qk[z, :, b * P:(b + 1) * P, c].rearrange("a p t -> p a t"),
                                     part[:, n % 2, z, :, :]).then_inc(s_out[n % 2], 16)
                    if n == 1:
                        for s in range(2):
                            sp.wait_ge(s_out[s], 32)
                    if n in (2, 4, 6):
                        load_head(sp, d, g, n // 2 - 1, n // 2 - 1)
            if not attend:
                plan_padding(sp, d, g, plan, range(E // 2))

        @block.gpsimd
        def _(pool):
            def both_parities(n):
                b, c = half(n)
                pool.wait_ge(s_num_in[b], 32)
                nc.gpsimd.tensor_tensor(num[:, b % 2, 0, c], num[:, b % 2, 0, c], num[:, b % 2, 1, c],
                                        ALU.add).then_inc(s_num, 1)

            for t in range(-4, groups):
                if last_part and live(t + 4):
                    both_parities(t + 4)
                if attend and live(t + 4):
                    pool.wait_ge(s_src[t + 4], 16)
                    x = g.x[:, cols(t + 4)]
                    nc.gpsimd.tensor_tensor(x, yb[:, cols(t + 4)], x, ALU.add).then_inc(s_new, 1)
                if not attend and live(t):
                    pool.wait_ge(s_pos, t + 1)
                    scatter_group(nc, pool, d, g, xn_rows, t)
                if attend and live(t):
                    for z in range(2):
                        pool.wait_ge(s_mid, 2 * t + z + 1)
                        nc.gpsimd.tensor_tensor(part[:, t % 2, z, 2, :], rest[:, t % 2, z, :],
                                                part[:, t % 2, z, 1, :], ALU.subtract).then_inc(s_part, 1)
            if not attend:
                pool.wait_ge(g.s_put, 16 * NT)

        @block.vector
        def _(dve):
            def reciprocals(b):
                dve.wait_ge(s_den_in[b], 32)
                if b >= 2:
                    dve.wait_ge(s_each, 2 * b - 2)
                nc.vector.tensor_tensor(den[:, b % 2, 0, :], den[:, b % 2, 0, :], den[:, b % 2, 1, :],
                                        ALU.add)
                dve.drain()
                nc.vector.reciprocal(rec[:, b % 2, :], den[:, b % 2, 0, :]).then_inc(s_rec, 1)

            def divide(n):
                b, c = half(n)
                dve.wait_ge(s_each, n + 1)
                dve.wait_ge(s_num, n + 1)
                if n >= 2:
                    dve.wait_ge(s_o, n - 1)
                nc.vector.tensor_tensor(aT[:, n % 2, :], num[:, b % 2, 0, c], psD[n % 2][:],
                                        ALU.mult).then_inc(s_aT, 1)

            def normalise(n):
                s = n % 2
                for j in range(4):
                    last = nc.vector.tensor_scalar(
                        xn[:, 4 * n + j, 0:D], xt[:, 4 * n + j, :],
                        mv[:, s, j, 0:1], rstd[:, s, j:j + 1], ALU.subtract, ALU.mult)
                last.then_inc(s_xn, 1)

            def new_x(n):
                s, x = n % 2, g.x[:, cols(n)]
                if first:
                    dve.wait_ge(s_src[n], 16)
                if attend:
                    dve.wait_ge(s_new, n + 1)
                if last_part:
                    dve.wait_ge(s_o, n + 1)
                    nc.vector.tensor_tensor(
                        xt[:, 4 * n:4 * n + 4, :], psO[s][:].rearrange("p (j d) -> p j d", d=D),
                        x.rearrange("p (j d) -> p j d", d=D), ALU.add).then_inc(s_x, 1)

            def rests(n):
                s = n % 2
                for z in range(2):
                    if n >= 2:
                        dve.wait_ge(s_part, 2 * n + z - 3)
                    dve.wait_ge(s_hi, 2 * n + z + 1)
                    nc.vector.scalar_tensor_tensor(out=rest[:, s, z, :], in0=psQ[z][s][:], scalar=scale[z],
                                                   in1=part[:, s, z, 0, :], op0=ALU.mult,
                                                   op1=ALU.subtract).then_inc(s_rest, 1)

            if first:
                dve.wait_ge(s_small, 3 * 16)
            if not attend:
                nc.vector.tensor_copy(xn[:, :, D:D + 1], g.const[:, C_TOK:C_TOK + NT].unsqueeze(2))
            iota = g.const[:, C_IOTA:C_IOTA + E].unsqueeze(1).to_broadcast([P, 4, E])

            for t in range(-3, groups + 1):
                turned, fresh = t + 1, t + 2
                choose = not attend and live(t)
                place = not attend and live(t - 1)
                s, o = t % 2, (t + 1) % 2
                if last_part and live(fresh):
                    divide(fresh)
                if live(turned):
                    normalise(turned)
                if not last_part and live(fresh):
                    new_x(fresh)
                if choose:
                    dve.wait_ge(s_used, t + 1)
                    nc.vector.tensor_tensor(
                        logit[:, s], psL[s][:, 0:4 * E].rearrange("p (j e) -> p j e", e=E),
                        g.br[:].unsqueeze(1).to_broadcast([P, 4, E]), ALU.add)
                dve.drain()
                if choose:
                    nc.vector.tensor_reduce(best[:, s], logit[:, s], AX.X, ALU.max)
                if last_part and live(t + 3) and (t + 3) % 2 == 0:
                    reciprocals((t + 3) // 2)
                if last_part and live(fresh):
                    new_x(fresh)
                dve.drain()
                if choose:
                    nc.vector.tensor_tensor(eq[:, s], logit[:, s],
                                            best[:, s].unsqueeze(2).to_broadcast([P, 4, E]), ALU.is_equal)
                if live(fresh):
                    for j in range(4):
                        nc.vector.bn_stats(stats[:, s, j, :], xt[:, 4 * fresh + j, :])
                if place:
                    dve.wait_ge(s_rank, t)
                    nc.vector.tensor_tensor(row[:, o], hot[:, o, :, 1:5].rearrange("p e j -> p j e"),
                                            psL[o][:, 4 * E:8 * E].rearrange("p (j e) -> p j e", e=E),
                                            ALU.mult).then_inc(s_read, 1)
                dve.drain()
                if place:
                    nc.vector.tensor_reduce(posf[:, o], row[:, o], AX.X, ALU.add)
                if choose:
                    nc.vector.tensor_tensor(eq[:, s], eq[:, s], iota, ALU.mult)
                if live(fresh):
                    for j in range(4):
                        nc.vector.bn_aggr(mv[:, s, j, :], stats[:, s, j, :])
                dve.drain()
                if live(fresh):
                    nc.vector.tensor_scalar(var[:, s, :], mv[:, s, :, 1], LN_EPS, None, ALU.add)\
                        .then_inc(s_var, 1)
                if place:
                    nc.vector.tensor_copy(g.pos[:, 4 * t - 4:4 * t], posf[:, o]).then_inc(s_pos, 1)
                if choose:
                    nc.vector.tensor_reduce(pick[:, s], eq[:, s], AX.X, ALU.min)
                    dve.drain()
                    nc.vector.tensor_tensor(hot[:, s, :, 1:5].rearrange("p e j -> p j e"), iota,
                                            pick[:, s].unsqueeze(2).to_broadcast([P, 4, E]), ALU.is_equal)
                    nc.vector.tensor_copy(hot[:, s, :, 0], upto[:, o, :, 4] if t else
                                          g.const[:, C_BASE:C_BASE + E])
                    dve.drain()
                    nc.vector.tensor_tensor_scan(
                        upto[:, s].rearrange("p e j -> p (e j)"), g.const[:, C_CARRY:C_CARRY + 5 * E],
                        hot[:, s].rearrange("p e j -> p (e j)"), 0.0, ALU.mult, ALU.add)\
                        .then_inc(s_upto, 1)
                if attend and live(t):
                    rests(t)
                if live(fresh):
                    dve.wait_ge(s_std, fresh + 1)
                    nc.vector.reciprocal(rstd[:, s, :], std[:, s, :])
                    dve.drain()
            if not attend:
                plan_tiles(nc, dve, g, plan)

        @block.tensor
        def _(pe):
            if first:
                pe.wait_ge(s_small, 3 * 16)

            def spread(n):
                b, s = n // 2, n % 2
                pe.wait_ge(s_rec, b + 1)
                if n >= 2:
                    pe.wait_ge(s_aT, n - 1)
                for j in range(4):
                    k = n % 2 * 4 + j
                    last = nc.tensor.matmul(psD[s][:, j * P:(j + 1) * P], pickhead[:, k * P:(k + 1) * P],
                                            rec[:, b % 2, :], start=True, stop=True)
                last.then_inc(s_each, 1)

            def project(n):
                s = n % 2
                pe.wait_ge(s_aT, n + 1)
                if n >= 2:
                    pe.wait_ge(s_x, n - 1)
                for j in range(4):
                    last = nc.tensor.matmul(psO[s][:, j * D:(j + 1) * D], aT[:, s, j * D:(j + 1) * D],
                                            g.wproj[:], start=True, stop=True)
                last.then_inc(s_o, 1)

            def turn(n):
                s = n % 2
                pe.wait_ge(s_xn, n + 1)
                if n >= 2:
                    pe.wait_ge(s_xT, n - 1)
                for j in range(4):
                    last = nc.tensor.transpose(psT[s][:, j * D:(j + 1) * D], xn[:, 4 * n + j, 0:D], g.ident)
                last.then_inc(s_tp, 1)

            def use(n):
                s = n % 2
                pe.wait_ge(s_xT, n + 1)
                if attend:
                    if n >= 2:
                        pe.wait_ge(s_rest, 2 * n - 2)
                    for z in range(2):
                        nc.tensor.matmul(psQ[z][s][:], g.wqkv[:, z * D:(z + 1) * D], xT[:, s, :],
                                         start=True, stop=True).then_inc(s_qk, 1)
                    if n >= 2:
                        pe.wait_ge(s_v, n - 1)
                    for j in range(4):
                        last = nc.tensor.matmul(psV[s][:, j * D:(j + 1) * D], xT[:, s, j * D:(j + 1) * D],
                                                g.wqkv[:, 2 * D:3 * D], start=True, stop=True)
                else:
                    if n >= 2:
                        pe.wait_ge(s_read, n - 1)
                    for j in range(4):
                        last = nc.tensor.matmul(psL[s][:, j * E:(j + 1) * E], xT[:, s, j * D:(j + 1) * D],
                                                g.wr[:], start=True, stop=True)
                last.then_inc(s_used, 1)

            def rank(n):
                s, at = n % 2, 4 * E
                pe.wait_ge(s_upto, n + 1)
                out = psL[s][:, at:at + 4 * E].rearrange("p (j e) -> p j e", e=E)
                nc.tensor.matmul(out, g.const[:, C_TRI:C_TRI + P],
                                 hot[:, s, :, 1:5].rearrange("p e j -> p j e"), start=True, stop=False)
                nc.tensor.matmul(out, g.const[:, C_ONE:C_ONE + P],
                                 upto[:, s, :, 0:4].rearrange("p e j -> p j e"), start=False,
                                 stop=True).then_inc(s_rank, 1)
                if n == groups - 1:
                    nc.tensor.matmul(psL[1 - s][:, 0:E], g.const[:, C_ONE:C_ONE + P], upto[:, s, :, 4],
                                     start=True, stop=True).then_inc(plan.s_cnt, 1)

            if last_part:
                pe.wait_ge(g.s_pick, 16)
            for t in range(-3, groups):
                if last_part and live(t + 2):
                    project(t + 2)
                if live(t + 1):
                    turn(t + 1)
                if last_part and live(t + 3):
                    spread(t + 3)
                if live(t + 1):
                    use(t + 1)
                if not attend and live(t):
                    rank(t)

        @block.scalar
        def _(act):
            for t in range(-3, groups + 1):
                n, s = t + 1, (t + 1) % 2
                if live(n):
                    act.wait_ge(s_tp, n + 1)
                    if n >= 2:
                        act.wait_ge(s_used, n - 1)
                    nc.scalar.copy(xT[:, s, :], psT[s][:]).then_inc(s_xT, 1)
                n, s = t, t % 2
                if attend and live(n):
                    for z in range(2):
                        act.wait_ge(s_qk, 2 * n + z + 1)
                        if n >= 2 and z == 0:
                            act.wait_ge(s_out[s], 32 * (n // 2))
                        nc.scalar.activation(part[:, s, z, 0, :], psQ[z][s][:], ACT.Copy,
                                             scale=scale[z]).then_inc(s_hi, 1)
                    act.wait_ge(s_used, n + 1)
                    b, k = n // 2, n % 2 * 4
                    nc.scalar.copy(g.v[:, b * HEADS:(b + 1) * HEADS, k:k + 4, :],
                                   psV[s][:].rearrange("p (j h e) -> p h j e", j=4, h=HEADS))\
                        .then_inc(s_v, 1)
                n, s = t + 2, t % 2
                if live(n):
                    act.wait_ge(s_var, n + 1)
                    nc.scalar.activation(std[:, s, :], var[:, s, :], ACT.Sqrt).then_inc(s_std, 1)
                n, s = t, t % 2
                if attend and live(n):
                    for z in range(2):
                        act.wait_ge(s_rest, 2 * n + z + 1)
                        nc.scalar.copy(part[:, s, z, 1, :], rest[:, s, z, :]).then_inc(s_mid, 1)
            if not attend:
                plan_padding(act, d, g, plan, range(E // 2, E))


def load_results(sp, d, to, s_got):
    y = d.y.rearrange("(p t) d -> p (t d)", p=P)
    for n in range(NT // 4):
        at = slice(n * HALF, (n + 1) * HALF)
        sp.dma_start(to[:, at], y[:, at]).then_inc(s_got[n], 16)


def phase_experts(nc, d, g, tag):
    row_len, to = ROW[tag], d.results[tag]
    with ExitStack() as ctx:
        m = Mem(nc, ctx)
        xs = m.sb(f"xs{tag}", [P, XBUF, row_len])
        if tag == "b":
            xb = m.sb("xb", [P, XBUF, D])
        ids = m.sb(f"ids{tag}", [P, XBUF], I32)
        xsT = m.sb(f"xsT{tag}", [P, 2, P])
        w1s = m.sb(f"w1s{tag}", [P, 2, W1])
        sig = m.sb(f"sig{tag}", [P, 2, HID])
        hid = m.sb(f"hid{tag}", [P, 2, HID])
        y = m.sb(f"y{tag}", [P, 2, D])
        warm = m.sb(f"warm{tag}", [1, 1])
        psA = [m.ps(f"psA{tag}{s}", [P, HID]) for s in range(2)]
        psG = [m.ps(f"psG{tag}{s}", [P, HID]) for s in range(2)]
        psY = [m.ps(f"psY{tag}{s}", [P, 512]) for s in range(2)]
        psX = m.ps(f"psX{tag}", [P, 512])
        S = {n: m.sem(f"s_{n}{tag}") for n in
             ("xt", "xsT", "w1s", "h", "sig", "hid", "id", "yp", "y", "go")}
        s_xs = [m.sem(f"s_xs{tag}{n}") for n in range(XBUF)]
        s_st = [m.sem(f"s_st{tag}{s}") for s in range(2)]
        block = ctx.enter_context(nc.Block())
        T = ET
        LOOPS = (T - 7) // XBUF
        AFTER = XBUF + XBUF * LOOPS

        def steps(eng, step):
            for i in range(1 - XBUF, XBUF):
                step(i, i, i, 0)
            with eng.Fori(0, LOOPS) as q:
                for r in range(XBUF, 2 * XBUF):
                    step(q * XBUF + r, r, None, q)
            for i in range(AFTER, T + 1):
                step(i, i, i, 0)

        def live(at, lag):
            return at is None or 0 <= at - lag < T

        def later(at, lag, n):
            return at is None or at - lag >= n

        @block.sync
        def _(sp):
            def step(i, r, at, q):
                if live(at, -3):
                    if later(at, -3, XBUF):
                        sp.wait_ge(S["xt"], i)
                        sp.wait_ge(S["id"], i)
                    n = (r + 3) % XBUF
                    row = sp.value_load(g.trow[0:1, bass.ds(i + 3, 1)], min_val=0,
                                        max_val=E * REGION + (SPARE - 1) * P)
                    sp.dma_start(xs[:, n, :], d.sorted[tag][bass.ds(row, P), :]).then_inc(s_xs[n], 16)
            steps(sp, step)

        @block.gpsimd
        def _(pool):
            def step(i, r, at, q):
                if live(at, 1):
                    s = (r + 1) % 2
                    pool.wait_ge(S["y"], i)
                    pool.sem_inc(S["go"], 1)
                    pool.indirect_dma_start(
                        out=to, in_=y[:, s, :], in_offset=None,
                        bounds_check=NTOK - 1, oob_is_err=False,
                        out_offset=bass.IndirectOffsetOnAxis(
                            ap=ids[:, (r + 3) % XBUF:(r + 3) % XBUF + 1], axis=0)).then_inc(s_st[s], 16)
            steps(pool, step)
            for s in range(2):
                pool.wait_ge(s_st[s], 16 * ((T + 1 - s) // 2))

        @block.tensor
        def _(pe):
            pe.wait_ge(g.s_w, 48)

            def step(i, r, at, q):
                s = r % 2
                if live(at, 0):
                    pe.wait_ge(S["xsT"], i + 1)
                    pe.wait_ge(S["w1s"], i + 1)
                    for a, (ps, used) in enumerate(((psG[s], "sig"), (psA[s], "hid"))):
                        if later(at, 0, 2):
                            pe.wait_ge(S[used], i - 1)
                        for c in range(4):
                            lo = (1 - a) * HID + c * P
                            last = nc.tensor.matmul(ps[:, c * P:(c + 1) * P], w1s[:, s, lo:lo + P],
                                                    xsT[:, s, :], start=True, stop=True)
                        last.then_inc(S["h"], 1)
                if live(at, -1):
                    pe.wait_ge(s_xs[(r + 1) % XBUF], 16 * (q + (r + 1) // XBUF + 1))
                    if later(at, -1, 1):
                        pe.wait_ge(S["xsT"], i + 1)
                    nc.tensor.transpose(psX[:, 0:P], xs[:, (r + 1) % XBUF, 0:D], g.ident)\
                        .then_inc(S["xt"], 1)
                if live(at, 1):
                    e = pe.value_load(g.eid[0:1, bass.ds(i - 1, 1)], min_val=0, max_val=E - 1)
                    pe.wait_ge(S["hid"], i)
                    if later(at, 1, 2):
                        pe.wait_ge(S["y"], i - 2)
                    for c in range(4):
                        last = nc.tensor.matmul(psY[1 - s][:, 0:D], hid[:, 1 - s, c * P:(c + 1) * P],
                                                g.w2[:, bass.ds(e * HID + c * P, P)],
                                                start=(c == 0), stop=(c == 3))
                    last.then_inc(S["yp"], 1)
            steps(pe, step)

        @block.vector
        def _(dve):
            dve.wait_ge(g.s_w, 48)
            nc.vector.tensor_scalar(g.b2[:], g.b2[:], 0.5, None, ALU.mult)
            dve.drain()

            def expert(i):
                return dve.value_load(g.eid[0:1, bass.ds(i, 1)], min_val=0, max_val=E - 1)

            def step(i, r, at, q):
                s = r % 2
                if live(at, -1):
                    e = expert(i + 1)
                    if later(at, -1, 2):
                        dve.wait_ge(S["h"], 2 * i)
                        dve.wait_ge(S["hid"], i)
                    nc.vector.tensor_copy(w1s[:, 1 - s, :], g.w1[:, bass.ds(e * W1, W1)])\
                        .then_inc(S["w1s"], 1)
                    dve.wait_ge(s_xs[(r + 1) % XBUF], 16 * (q + (r + 1) // XBUF + 1))
                    if later(at, -1, XBUF):
                        dve.wait_ge(s_st[1 - s], 16 * (2 * q + (r - 3) // 2 + 1))
                    if tag == "b":
                        nc.vector.tensor_tensor(xb[:, (r + 1) % XBUF, :], g.b2[:, bass.ds(e * D, D)],
                                                xs[:, (r + 1) % XBUF, D + 1:], ALU.add)
                    nc.vector.tensor_copy(ids[:, (r + 1) % XBUF:(r + 1) % XBUF + 1],
                                          xs[:, (r + 1) % XBUF, D:D + 1]).then_inc(S["id"], 1)
                if live(at, 1):
                    if tag == "a":
                        e = expert(i - 1)
                        more = g.b2[:, bass.ds(e * D, D)]
                    else:
                        more = xb[:, (r + 3) % XBUF, :]
                        dve.drain()
                    dve.wait_ge(S["yp"], i)
                    if later(at, 1, 2):
                        dve.wait_ge(s_st[1 - s], 16 * (2 * q + (r - 3) // 2 + 1))
                    last = nc.vector.scalar_tensor_tensor(
                        out=y[:, 1 - s, :], in0=psY[1 - s][:, 0:D], scalar=0.5, in1=more,
                        op0=ALU.mult, op1=ALU.add)
                    last.then_inc(S["y"], 1)
                if live(at, 0):
                    if later(at, 0, 2):
                        dve.wait_ge(S["yp"], i - 1)
                    for c in range(4):
                        if c == 0:
                            dve.wait_ge(S["h"], 2 * i + 2)
                            dve.wait_ge(S["sig"], i + 1)
                        last = nc.vector.scalar_tensor_tensor(
                            out=hid[:, s, c * P:(c + 1) * P], in0=psA[s][:, c * P:(c + 1) * P],
                            scalar=w1s[:, s, 2 * HID + c:2 * HID + c + 1],
                            in1=sig[:, s, c * P:(c + 1) * P], op0=ALU.add, op1=ALU.mult)
                    last.then_inc(S["hid"], 1)
            steps(dve, step)

        @block.scalar
        def _(act):
            nc.scalar.activation(warm[:], g.const[0:1, 0:1], ACT.Sigmoid)

            def step(i, r, at, q):
                s = r % 2
                if live(at, 0):
                    act.wait_ge(S["h"], 2 * i + 1)
                    if later(at, 0, 2):
                        act.wait_ge(S["hid"], i - 1)
                    for c in range(4):
                        b = 2 * HID + 4 + c
                        last = nc.scalar.activation(sig[:, s, c * P:(c + 1) * P],
                                                    psG[s][:, c * P:(c + 1) * P], ACT.Sigmoid,
                                                    bias=w1s[:, s, b:b + 1])
                    last.then_inc(S["sig"], 1)
                if live(at, -1):
                    act.wait_ge(S["xt"], i + 2)
                    if later(at, -1, 2):
                        act.wait_ge(S["h"], 2 * i)
                    nc.scalar.copy(xsT[:, 1 - s, :], psX[:, 0:P]).then_inc(S["xsT"], 1)
            steps(act, step)


def load_sums(sp, d, g, b):
    sums = d.sums.rearrange("(b h) a e t -> b a h e t", h=HEADS)
    for a in range(2):
        sp.dma_start(g.den[:, b % 2, a, :], sums[b, a, :, DH, :].rearrange("h (j q) -> h j q", q=P))\
            .then_inc(g.s_den_in[b], 16)
        sp.dma_start(g.num[:, b % 2, a, :], sums[b, a, :, 0:DH, :]).then_inc(g.s_num_in[b], 16)


def load_head(sp, d, g, head, b):
    rows = bass.ds(head * DH, DH)
    for a in range(3):
        at = slice(a * 3 * DH, (a + 1) * 3 * DH)
        sp.dma_start(g.qop[b][at, :], d.qk[0, a, rows, :].unsqueeze(0).to_broadcast([3, DH, L])
                     ).then_inc(g.s_op[b], 16)
        sp.dma_start(g.kop[b][at, :], d.qk[1, :, rows, :]).then_inc(g.s_op[b], 16)


def phase_attention(nc, d, g):
    with ExitStack() as ctx:
        m = Mem(nc, ctx)
        qop, kop, s_op, s_init = g.qop, g.kop, g.s_op, g.s_init
        prob = [m.sb(f"prob{s}", [P, KT * PBLK]) for s in range(2)]
        vst = [m.sb(f"vst{s}", [P, KT, VW]) for s in range(2)]
        nmax = [m.sb(f"nmax{s}", [P, KT]) for s in range(2)]
        res = m.sb("res", [P, KT])
        none = m.sb("none", [P, KT])
        mpart = [m.sb(f"mpart{s}", [P, 4, KT], BF16) for s in range(2)]
        mrow = [m.sb(f"mrow{s}", [P, 4 * KT], BF16) for s in range(2)]
        osum = [m.sb(f"osum{s}", [P, HALF]) for s in range(2)]
        psS = [m.ps(f"psS{s}", [P, 2, HALF]) for s in range(2)]
        psE = [m.ps(f"psE{s}", [P, HALF]) for s in range(3)]
        psV = m.ps("psV", [P, HALF])
        s_mr = [m.sem(f"s_mr{n}") for n in range(NBUF)]
        s_one = m.sem("s_one")
        s_s, s_max = m.sem("s_s"), m.sem("s_max")
        s_mp, s_mt = m.sem("s_mp"), m.sem("s_mt")
        s_t, s_exp = m.sem("s_t"), m.sem("s_exp")
        s_diag, s_vst = m.sem("s_diag"), m.sem("s_vst")
        s_pv, s_ev = m.sem("s_pv"), m.sem("s_ev")
        s_os = g.s_os
        block = ctx.enter_context(nc.Block())
        N = NHEAD
        BANK = [n % 3 for n in range(16)]
        BANK_AGE = [min(a for a in range(1, 17) if BANK[(n - a) % 16] == BANK[n]) for n in range(16)]

        def steps(eng, step, lo, hi):
            for i in range(lo, NBUF):
                step(i, i, i, 0)
            with eng.Fori(0, N // NBUF - 2) as q:
                for k in range(NBUF, 2 * NBUF):
                    step(q * NBUF + k, k, None, q)
            for i in range(N - NBUF, hi):
                step(i, i, i, 0)

        def live(at, head):
            return at is None or 0 <= at + head < N

        def later(at, head, n):
            return at is None or at + head >= n


        def filled(q, r, head):
            return q + (r + head) // NBUF + 1

        @block.sync
        def _(sp):
            def step(i, r, at, q):
                if live(at, 3) and later(at, 0, 0):
                    if later(at, 3, NBUF):
                        sp.wait_ge(s_t, 16 * i)
                    load_head(sp, d, g, i + 3, (r + 3) % NBUF)
                if live(at, -2):
                    sp.wait_ge(s_ev, i - 1)
                    for j in range(4):
                        sp.dma_start(d.sums[bass.ds(i - 2, 1), j // 2, :,
                                            (j % 2) * HALF:(j % 2 + 1) * HALF].squeeze(),
                                     osum[r % 2][32 * j:32 * j + VW, :]).then_inc(s_os[r % 2], 16)
                if live(at, 1):
                    b = (r + 1) % NBUF
                    sp.wait_ge(s_mt, i + 2)
                    for u in range(4):
                        sp.dma_start(qop[b][MAX0:TROWS, :].rearrange("a (t q) -> a t q", q=P)
                                     [:, :, 32 * u:32 * u + 32],
                                     mrow[(r + 1) % 2][32 * u:32 * u + 3 * KT, :]).then_inc(s_mr[b], 16)
                if at == N - 3:
                    for s in range(2):
                        sp.wait_ge(s_os[s], 64 * (N // 2 - 3 + s))
                    sp.dma_start(g.pickhead[:], d.pickhead).then_inc(g.s_pick, 16)
                    for batch in range(2):
                        load_sums(sp, d, g, batch)
            for s in range(2):
                sp.wait_ge(g.s_out[s], 32 * (NT // 8))
            steps(sp, step, -3, N + 2)

        @block.tensor
        def _(pe):
            pe.wait_ge(s_init, 16 * 2 * NBUF)
            pe.wait_ge(s_one, 5)

            def step(i, r, at, q):
                for kt in range(KT):
                    for half in range(2):
                        cols = slice(half * HALF, (half + 1) * HALF)
                        if live(at, 0):
                            b, n = r % NBUF, 2 * kt + half
                            if n == 0:
                                pe.wait_ge(s_mr[b], 64 * filled(q, r, 0))
                            if later(at, 0, 1) or n >= BANK_AGE[n]:
                                pe.wait_ge(s_exp, 16 * i + n + 1 - BANK_AGE[n])
                            nc.tensor.matmul(psE[BANK[n]][:], kop[b][0:TROWS, kt * P:(kt + 1) * P],
                                             qop[b][0:TROWS, cols], start=True, stop=True).then_inc(s_t, 1)
                        if live(at, 2):
                            b = (r + 2) % NBUF
                            if kt == 0 and half == 0:
                                pe.wait_ge(s_op[b], 96 * filled(q, r, 2))
                            if half == 0 and (later(at, 2, 1) or kt >= 2):
                                pe.wait_ge(s_max, 8 * (i + 2) + kt - 1)
                            last = nc.tensor.matmul(psS[kt % 2][:, half, :],
                                                    qop[b][0:SROWS, kt * P:(kt + 1) * P],
                                                    kop[b][0:SROWS, cols], start=True, stop=True)
                            if half == 1:
                                last.then_inc(s_s, 1)
                    if kt % 2 == 1 and live(at, -1):
                        if kt == 1:
                            pe.wait_ge(s_vst, i)
                            if later(at, -1, 1):
                                pe.wait_ge(s_ev, i - 1)
                        if kt in (1, 5):
                            pe.wait_ge(s_diag, 2 * i - 1 + kt // 4)
                            pe.wait_ge(s_exp, 16 * i - 8 + 8 * (kt // 4))
                        for j in range(4):
                            k, half = kt - 1 + j // 2, j % 2
                            last = nc.tensor.matmul(
                                psV[32 * j:32 * j + VW, :], vst[(r + 1) % 2][:, k, :],
                                prob[(r + 1) % 2][:, k * PBLK + half * HALF:k * PBLK + (half + 1) * HALF],
                                start=(kt == 1), stop=(kt == 7))
                        if kt == 7:
                            last.then_inc(s_pv, 1)

            steps(pe, step, -2, N + 1)

        @block.vector
        def _(dve):
            nc.vector.memset(psV[:], 0.0).then_inc(s_one, 1)
            for s in range(2):
                nc.vector.memset(vst[s][:, :, DH:VW], 1.0).then_inc(s_one, 1)
            for s in range(2):
                nc.vector.memset(mpart[s][:, 3, :], 0.0).then_inc(s_one, 1)

            def step(i, r, at, q):
                for qt in range(KT):
                    if qt == 2 and live(at, 1):
                        dve.wait_ge(s_mp, i + 2)
                        if later(at, 1, 2):
                            dve.wait_ge(s_mr[(r + 3) % NBUF], 64 * filled(q, r, -1))
                        nc.vector.transpose(mrow[(r + 1) % 2][:],
                                            mpart[(r + 1) % 2][:].rearrange("p a t -> p (a t)"))\
                            .then_inc(s_mt, 1)
                    if live(at, 2):
                        dve.wait_ge(s_s, 8 * (i + 2) + qt + 1)
                        if qt == 0 and later(at, 2, 2):
                            dve.wait_ge(s_mp, i + 1)
                        nc.vector.tensor_reduce(nmax[r % 2][:, qt:qt + 1], psS[qt % 2][:], AX.XY, ALU.max,
                                                negate=True).then_inc(s_max, 1)
            steps(dve, step, -2, 63)

        @block.scalar
        def _(act):
            def step(i, r, at, q):
                for n in range(16):
                    if live(at, 0):
                        act.wait_ge(s_t, 16 * i + n + 1)
                        if n == 0 and later(at, 0, 2):
                            act.wait_ge(s_pv, i - 1)
                        kt, half = n // 2, n % 2
                        lo = kt * PBLK + half * HALF
                        nc.scalar.activation(prob[r % 2][:, lo:lo + HALF], psE[BANK[n]][:],
                                             ACT.Exp).then_inc(s_exp, 1)
                    if n == 0 and live(at, -2):
                        act.wait_ge(s_pv, i - 1)
                        if later(at, -2, 2):
                            act.wait_ge(s_os[r % 2], 64 * (2 * q + r // 2 - 1))
                        nc.scalar.copy(osum[r % 2][:], psV[:]).then_inc(s_ev, 1)
            steps(act, step, -1, 66)

        @block.gpsimd
        def _(pool):
            pool.wait_ge(s_one, 5)
            nc.gpsimd.memset(none[:], 0.0)
            x = g.x[:].rearrange("p (t d) -> p t d", d=D)
            nc.gpsimd.tensor_tensor(x, x, g.bproj[:].unsqueeze(1).to_broadcast([P, NT, D]), ALU.add)
            pool.drain()
            diag = g.const[:, C_DIAG:C_DIAG + KT * P].rearrange("p (k q) -> p k q", q=P)

            def step(i, r, at, q):
                if live(at, 1):
                    mp, nm = mpart[(r + 1) % 2], nmax[(r + 1) % 2]
                    pool.wait_ge(s_max, 8 * (i + 2))
                    if later(at, 1, 2):
                        pool.wait_ge(s_mt, i)
                    if later(at, 0, 2):
                        pool.wait_ge(s_pv, i - 1)
                    nc.gpsimd.tensor_tensor(mp[:, 0, :], nm[:], none[:], ALU.add)
                    pool.drain()
                    nc.gpsimd.tensor_tensor(res[:], nm[:], mp[:, 0, :], ALU.subtract)
                    pool.drain()
                    nc.gpsimd.tensor_copy(mp[:, 1, :], res[:])
                    pool.drain()
                    nc.gpsimd.tensor_tensor(mp[:, 2, :], res[:], mp[:, 1, :], ALU.subtract).then_inc(s_mp, 1)
                if live(at, 0):
                    if not live(at, 1):
                        pool.wait_ge(s_pv, i - 1)
                    nc.gpsimd.tensor_copy(
                        vst[r % 2][:, :, 0:DH].unsqueeze(1),
                        g.v[:, bass.ds(i, 1), :, :]).then_inc(s_vst, 1)
                    for h in range(2):
                        pool.wait_ge(s_exp, 16 * i + 8 * (h + 1))
                        dst = diag_blocks(prob[r % 2], h)
                        nc.gpsimd.tensor_tensor(dst, dst, diag[:, 4 * h:4 * h + 4, :],
                                                ALU.mult).then_inc(s_diag, 1)

            def diag_blocks(pr, h):
                full = pr[:, 0:P]
                return bass.AP(tensor=full.tensor, offset=4 * h * (PBLK + P),
                               ap=[list(full.ap[0]), [PBLK + P, 4], [1, P]])
            steps(pool, step, -1, 64)


class Names:
    pass


def build(nc, ins, out):
    d, g = Names(), Names()
    d.x, d.w_qkv, d.w_proj, d.b_proj, d.router_w, d.router_b = ins[0:6]
    d.w1, d.w2, d.b2, d.const, d.padding, d.pickhead, d.qbias, d.kbias = ins[6:14]
    d.sorted = {turn: nc.dram_tensor(f"sorted_{turn}", (E * REGION + SPARE * P, ROW[turn]), F32,
                                     kind="Internal").ap() for turn in "ab"}
    d.y = nc.dram_tensor("results", (NTOK, D), F32, kind="Internal").ap()
    d.results = {"a": d.y, "b": out}
    d.sums = nc.dram_tensor("weighted_sums", (NHEAD, 2, VW, L), F32, kind="Internal").ap()
    d.qk = nc.dram_tensor("qk_parts", (2, 3, NHEAD * DH, L), BF16, kind="Internal").ap()
    with ExitStack() as ctx:
        m = Mem(nc, ctx)
        g.x = m.sb("x", [P, NT * D])
        g.const = m.sb("const", [P, C_END])
        g.ident = g.const[:, C_ID:C_ID + P]
        g.wr = m.sb("wr", [P, E])
        g.br = m.sb("br", [P, E])
        g.wqkv = m.sb("wqkv", [P, 3 * D])
        g.wproj = m.sb("wproj", [P, D])
        g.bproj = m.sb("bproj", [P, D])
        g.s_spare, g.s_later = m.sem("s_spare"), m.sem("s_later")
        g.pos = m.sb("pos", [P, NT], I32)
        g.eid = m.sb("eid", [1, ET], I32)
        g.trow = m.sb("trow", [1, ET], I32)

        def experts_memory(tag, ectx):
            em = Mem(nc, ectx)
            g.w1, g.w2 = em.sb(f"w1{tag}", [P, E * W1]), em.sb(f"w2{tag}", [P, E * HID])
            g.b2 = em.sb(f"b2{tag}", [P, E * D])
            g.s_w = em.sem(f"s_w{tag}")
            g.s_put = em.sem(f"s_put{tag}")
            g.turn = tag

        with ExitStack() as ectx:
            experts_memory("a", ectx)
            phase_tokens(nc, d, g, "first")
            phase_experts(nc, d, g, "a")
        g.num, g.den = m.sb("num", [P, 2, 2, L]), m.sb("den", [P, 2, 2, P])
        g.pickhead = m.sb("pickhead", [P, KT * P])
        g.s_num_in = [m.sem(f"s_num_in{b}") for b in range(B)]
        g.s_den_in = [m.sem(f"s_den_in{b}") for b in range(B)]
        g.s_os = [m.sem(f"s_os{s}") for s in range(2)]
        g.s_pick = m.sem("s_pick")
        with ExitStack() as actx:
            am = Mem(nc, actx)
            g.v = am.sb("v", [P, NHEAD, KT, DH])
            g.qop = [am.sb(f"qop{n}", [TROWS, L], BF16) for n in range(NBUF)]
            g.kop = [am.sb(f"kop{n}", [TROWS, L], BF16) for n in range(NBUF)]
            g.s_op = [am.sem(f"s_op{n}") for n in range(NBUF)]
            g.s_init = am.sem("s_init")
            g.s_out = [am.sem(f"s_out{s}") for s in range(2)]
            phase_tokens(nc, d, g, "attend")
            phase_attention(nc, d, g)
        with ExitStack() as ectx:
            experts_memory("b", ectx)
            phase_tokens(nc, d, g, "last")
            phase_experts(nc, d, g, "b")


def kernel(L0_attn_x, L0_attn_w_qkv, L0_attn_w_proj, L0_attn_b_proj, L0_ffn_router_w, L0_ffn_router_b,
           L0_ffn_w1, L0_ffn_b1, L0_ffn_w2, L0_ffn_b2):
    import numpy as np
    import ml_dtypes
    import concourse.bacc as bacc
    from concourse.bass_utils import run_bass_kernel_spmd

    bf16 = ml_dtypes.bfloat16
    phi = np.float32((1.0 + np.sqrt(5.0)) / 2.0)
    pos = (np.arange(L, dtype=np.float32) * phi) % np.float32(1.0)
    order = np.argsort(pos, kind="stable")
    p = pos[order]

    def parts(a):
        hi = a.astype(bf16)
        mid = (a - hi.astype(np.float32)).astype(bf16)
        lo = (a - hi.astype(np.float32) - mid.astype(np.float32)).astype(bf16)
        return hi, mid, lo

    tile = np.arange(L) // P
    qbias = np.zeros((6, KT, L), bf16)
    kbias = np.zeros((6 * KT + 3, L), bf16)
    for t in range(KT):
        sign = np.where(tile <= t, np.float32(1), np.float32(-1))
        for a, part in enumerate(parts(p)):
            qbias[a, t] = (sign * part.astype(np.float32)).astype(bf16)
            qbias[3 + a, t] = (-sign).astype(bf16)
            kbias[a * KT + t] = (tile == t).astype(bf16)
            kbias[(3 + a) * KT + t] = np.where(tile == t, part.astype(np.float32), np.float32(0)).astype(bf16)
    kbias[6 * KT:] = np.ones((3, L), bf16)

    const = np.zeros((P, C_END), np.float32)
    const[:, C_ID:C_ID + P] = np.eye(P)
    const[:, C_TRI:C_TRI + P] = np.triu(np.ones((P, P)), 1)
    const[:, C_ONE:C_ONE + P] = 1.0
    pickhead = np.zeros((HEADS, KT, KT, HEADS, DH), np.float32)
    for h in range(HEADS):
        for k in range(KT):
            pickhead[h, k, k, h] = 1.0
    padding = np.zeros(((E + SPARE) * P, ROW["b"]), np.float32)
    padding[:, D] = NTOK + np.arange((E + SPARE) * P)
    for t in range(KT):
        pt = p[t * P:(t + 1) * P].astype(np.float64)
        const[:, C_DIAG + t * P:C_DIAG + (t + 1) * P] = np.exp(-2.0 * np.maximum(0.0, pt[None, :] - pt[:, None]))
    const[:, C_IOTA:C_IOTA + E] = np.arange(E) - E
    const[0, C_BASE:C_BASE + E] = np.arange(E) * REGION
    const[:, C_CARRY:C_CARRY + 5 * E] = np.tile([0.0, 1.0, 1.0, 1.0, 1.0], E)
    const[:, C_TOK:C_TOK + NT] = np.arange(P)[:, None] * NT + np.arange(NT)
    const[:, C_TILE:C_TILE + ET] = np.arange(ET) * P

    def tiled(a):
        return np.ascontiguousarray(a.reshape(NT, P, D).transpose(1, 0, 2)).reshape(P, NT * D)

    arrays = {
        "x": tiled(np.asarray(L0_attn_x)[:, order, :]),
        "w_qkv": np.asarray(L0_attn_w_qkv), "w_proj": np.asarray(L0_attn_w_proj),
        "b_proj": np.asarray(L0_attn_b_proj),
        "router_w": np.asarray(L0_ffn_router_w), "router_b": np.asarray(L0_ffn_router_b),
        "w1": np.concatenate([np.asarray(L0_ffn_w1).transpose(1, 0, 2),
                              np.asarray(L0_ffn_b1).reshape(E, 2 * HID // P, P).transpose(2, 0, 1)],
                             axis=2).reshape(P, E * W1),
        "w2": np.ascontiguousarray(np.asarray(L0_ffn_w2).reshape(E, HID // P, P, D).transpose(2, 0, 1, 3))
                .reshape(P, E * HID),
        "b2": np.asarray(L0_ffn_b2).reshape(E * D),
        "const": const, "padding": padding, "pickhead": pickhead.reshape(P, KT * P),
        "qbias": qbias.reshape(6 * KT, L), "kbias": kbias,
    }
    arrays = {f"in_{n}": np.ascontiguousarray(a) for n, a in arrays.items()}
    nc = bacc.Bacc("TRN2", target_bir_lowering=False, num_devices=1)
    ins = [nc.dram_tensor(n, a.shape, mybir.dt.from_np(a.dtype), kind="ExternalInput").ap()
           for n, a in arrays.items()]
    out = nc.dram_tensor("out_x", (NTOK, D), F32, kind="ExternalOutput").ap()
    build(nc, ins, out)
    r = run_bass_kernel_spmd(nc, [arrays], core_ids=[0])
    y = np.asarray(r.results[0]["out_x"]).reshape(P, NT, D).transpose(1, 0, 2).reshape(B, L, D)
    back = np.empty_like(order)
    back[order] = np.arange(L)
    return y[:, back, :]
```
